# Optimizing a Trainium2 kernel written in Bass

```python
import numpy as np
import jax
import jax.numpy as jnp

def _softmax(x, axis=-1):
    return jax.nn.softmax(x, axis=axis)

def _gelu(x):
    return jax.nn.gelu(x, approximate=True)

def _silu(x):
    return jax.nn.silu(x)

def _sigmoid(x):
    return jax.nn.sigmoid(x)

def _layernorm(x, axis=-1, eps=1e-05):
    m = jnp.mean(x, axis=axis, keepdims=True)
    v = jnp.var(x, axis=axis, keepdims=True)
    return (x - m) / jnp.sqrt(v + eps)

def _scatter_add(tgt, idx, src, axis=0):
    return tgt.at[idx].add(src)

def _segment_sum(src, seg, n):
    return jax.ops.segment_sum(src, seg, n)
kernel_name = 'mk_adaln_d1_jaxref_r8_37ece9'

def setup_inputs(seed: int=0):
    np.random.seed(seed)
    _w = jnp.asarray

    def _L0_attn_setup():
        import jax, jax.numpy as jnp
        import numpy as np
        INFTY_APPROX = 1e+30
        ROTARY_BASE = 10000.0
        D_HEAD = 128

        def rope(x, base=ROTARY_BASE):
            *_, length, width = x.shape
            half = width // 2
            positions = jnp.arange(length)[:, None].astype(jnp.float32)
            ang_freqs = jnp.power(base, -jnp.arange(half) / half)[None, :]
            radians = positions * ang_freqs
            cos = jnp.cos(radians).astype(x.dtype)[None, None]
            sin = jnp.sin(radians).astype(x.dtype)[None, None]
            even, odd = jnp.split(x, 2, axis=-1)
            return jnp.concatenate([even * cos - odd * sin, even * sin + odd * cos], axis=-1)
        key = jax.random.key(seed)
        ks = jax.random.split(key, 5)
        B, T, M, H, D = (2, 256, 128, 8, D_HEAD)
        x = jax.random.normal(ks[0], (B, T, M), dtype=jnp.float32)
        scale = M ** (-0.5)
        wq = jax.random.normal(ks[1], (M, H, D), dtype=jnp.float32) * scale
        wk = jax.random.normal(ks[2], (M, H, D), dtype=jnp.float32) * scale
        wv = jax.random.normal(ks[3], (M, H, D), dtype=jnp.float32) * scale
        wo = jax.random.normal(ks[4], (H, D, M), dtype=jnp.float32) * scale
        return {'x': x, 'wq': wq, 'wk': wk, 'wv': wv, 'wo': wo}
    _L0_attn_in = _L0_attn_setup()

    def _L0_ffn_setup():
        import jax, jax.numpy as jnp
        import numpy as np
        DIM = 128
        DEPTH = 6
        HEADS = 16
        DIM_HEAD = 64
        WINDOW = 32
        INNER = HEADS * DIM_HEAD
        DIM_INNER = int(DIM * 4 * 2 / 3)
        QK_SCALE = 8.0

        def shift_tokens(t):
            a, s = jnp.split(t, 2, -1)
            s = jnp.pad(s, ((0, 0), (1, 0), (0, 0)))[:, :-1]
            return jnp.concatenate([a, s], -1)

        def l2norm(t):
            return t / jnp.maximum(jnp.linalg.norm(t, axis=-1, keepdims=True), 1e-12)

        def rotate_half(x):
            x1, x2 = jnp.split(x, 2, -1)
            return jnp.concatenate([-x2, x1], -1)

        def rotary_tables(n):
            half = jnp.arange(0, DIM_HEAD, 2, dtype=jnp.float32)
            inv_freq = 1.0 / 10000.0 ** (half / DIM_HEAD)
            t = jnp.arange(n, dtype=jnp.float32)
            freqs = t[:, None] * inv_freq[None, :]
            freqs = jnp.concatenate([freqs, freqs], -1)
            base_scale = (half + 0.4 * DIM_HEAD) / (1.4 * DIM_HEAD)
            power = (t - n // 2) / (WINDOW // 2)
            scale = base_scale[None, :] ** power[:, None]
            scale = jnp.concatenate([scale, scale], -1)
            return (freqs, scale)

        def local_attention(q, k, v):
            b, h, n, d = q.shape
            w = WINDOW
            nw = n // w
            bq = q.reshape(b, h, nw, w, d)
            bk = k.reshape(b, h, nw, w, d)
            bv = v.reshape(b, h, nw, w, d)

            def look(t):
                p = jnp.pad(t, ((0, 0), (0, 0), (1, 0), (0, 0), (0, 0)))
                return jnp.concatenate([p[:, :, :nw], p[:, :, 1:]], axis=3)
            bk2, bv2 = (look(bk), look(bv))
            seq = jnp.arange(n).reshape(nw, w)
            seq_p = jnp.pad(seq, ((1, 0), (0, 0)), constant_values=-1)
            jt = jnp.concatenate([seq_p[:nw], seq_p[1:]], axis=1)
            it = seq[:, :, None]
            jb = jt[:, None, :]
            mask = (it < jb) | (it > jb + w) | (jb == -1)
            sim = jnp.einsum('bhwie,bhwje->bhwij', bq, bk2) * QK_SCALE
            sim = jnp.where(mask, -jnp.finfo(sim.dtype).max, sim)
            attn = jax.nn.softmax(sim, -1)
            out = jnp.einsum('bhwij,bhwje->bhwie', attn, bv2)
            return out.reshape(b, h, n, d)

        def attn_layer(x, Wqkv, qs, ksc, Wo):
            b, n, _ = x.shape
            qkv = x @ Wqkv
            q, k, v = jnp.split(qkv, 3, -1)
            sh = lambda t: t.reshape(b, n, HEADS, DIM_HEAD).transpose(0, 2, 1, 3)
            q, k, v = (sh(q), sh(k), sh(v))
            q = l2norm(q) * qs
            k = l2norm(k) * ksc
            freqs, scale = rotary_tables(n)
            cos, sin = (jnp.cos(freqs), jnp.sin(freqs))
            q = q * cos * scale + rotate_half(q) * sin * scale
            inv = 1.0 / scale
            k = k * cos * inv + rotate_half(k) * sin * inv
            out = local_attention(q, k, v)
            out = out.transpose(0, 2, 1, 3).reshape(b, n, INNER)
            return out @ Wo

        def ffn_layer(x, g, bln, W1, b1, W2, b2):
            mu = x.mean(-1, keepdims=True)
            var = ((x - mu) ** 2).mean(-1, keepdims=True)
            xn = (x - mu) / jnp.sqrt(var + 1e-05) * g + bln
            hg = xn @ W1 + b1
            a, gate = jnp.split(hg, 2, -1)
            return a * jax.nn.gelu(gate, approximate=False) @ W2 + b2
        key = jax.random.key(seed)
        ks = jax.random.split(key, 8)
        B, N = (2, 256)
        init = lambda k, shape: jax.random.normal(k, shape, jnp.float32) * 0.02
        return {'x': jax.random.normal(ks[0], (B, N, DIM), jnp.float32), 'Wqkv': init(ks[1], (DEPTH, DIM, 3 * INNER)), 'q_scale': jnp.ones((DEPTH, DIM_HEAD), jnp.float32), 'k_scale': jnp.ones((DEPTH, DIM_HEAD), jnp.float32), 'Wo': init(ks[2], (DEPTH, INNER, DIM)), 'ln_g': jnp.ones((DEPTH, DIM), jnp.float32), 'ln_b': jnp.zeros((DEPTH, DIM), jnp.float32), 'W1': init(ks[3], (DEPTH, DIM, 2 * DIM_INNER)), 'b1': jnp.zeros((DEPTH, 2 * DIM_INNER), jnp.float32), 'W2': init(ks[4], (DEPTH, DIM_INNER, DIM)), 'b2': jnp.zeros((DEPTH, DIM), jnp.float32)}
    _L0_ffn_in = _L0_ffn_setup()
    _L0_c = _w((lambda *s: np.random.randn(*s).astype(np.float32) * 0.05)(8, 128))
    _L0_wmod = _w((lambda *s: np.random.randn(*s).astype(np.float32) * 0.05)(128, 6 * 128) * 128 ** (-0.5))
    _d = {'L0_attn_x': _L0_attn_in['x'], 'L0_attn_wq': _L0_attn_in['wq'], 'L0_attn_wk': _L0_attn_in['wk'], 'L0_attn_wv': _L0_attn_in['wv'], 'L0_attn_wo': _L0_attn_in['wo'], 'L0_ffn_Wqkv': _L0_ffn_in['Wqkv'], 'L0_ffn_q_scale': _L0_ffn_in['q_scale'], 'L0_ffn_k_scale': _L0_ffn_in['k_scale'], 'L0_ffn_Wo': _L0_ffn_in['Wo'], 'L0_ffn_ln_g': _L0_ffn_in['ln_g'], 'L0_ffn_ln_b': _L0_ffn_in['ln_b'], 'L0_ffn_W1': _L0_ffn_in['W1'], 'L0_ffn_b1': _L0_ffn_in['b1'], 'L0_ffn_W2': _L0_ffn_in['W2'], 'L0_ffn_b2': _L0_ffn_in['b2'], 'L0_c': _L0_c, 'L0_wmod': _L0_wmod}
    _x0 = _d['L0_attn_x']
    _d['L0_attn_x'] = jax.random.normal(jax.random.fold_in(jax.random.key(seed), 1), (8, 256, 128), dtype=_x0.dtype)
    del _x0
    return _d

def reference(L0_attn_x, L0_attn_wq, L0_attn_wk, L0_attn_wv, L0_attn_wo, L0_ffn_Wqkv, L0_ffn_q_scale, L0_ffn_k_scale, L0_ffn_Wo, L0_ffn_ln_g, L0_ffn_ln_b, L0_ffn_W1, L0_ffn_b1, L0_ffn_W2, L0_ffn_b2, L0_c, L0_wmod):

    def _L0_attn_ref(x, wq, wk, wv, wo):
        import jax, jax.numpy as jnp
        import numpy as np
        INFTY_APPROX = 1e+30
        ROTARY_BASE = 10000.0
        D_HEAD = 128

        def rope(x, base=ROTARY_BASE):
            *_, length, width = x.shape
            half = width // 2
            positions = jnp.arange(length)[:, None].astype(jnp.float32)
            ang_freqs = jnp.power(base, -jnp.arange(half) / half)[None, :]
            radians = positions * ang_freqs
            cos = jnp.cos(radians).astype(x.dtype)[None, None]
            sin = jnp.sin(radians).astype(x.dtype)[None, None]
            even, odd = jnp.split(x, 2, axis=-1)
            return jnp.concatenate([even * cos - odd * sin, even * sin + odd * cos], axis=-1)
        B, T, M = x.shape
        q = jnp.einsum('bim,mhd->bhid', x, wq)
        k = jnp.einsum('bim,mhd->bhid', x, wk)
        v = jnp.einsum('bim,mhd->bhid', x, wv)
        q = rope(q)
        k = rope(k)
        s = jnp.einsum('bhid,bhjd->bhij', q, k) / jnp.asarray(D_HEAD, q.dtype)
        i = jnp.arange(T)[:, None]
        j = jnp.arange(T)[None, :]
        mask = (i < j)[None, None]
        s = s - jnp.asarray(INFTY_APPROX, s.dtype) * mask
        p = jax.nn.softmax(s, axis=-1)
        o = jnp.einsum('bhij,bhjd->bhid', p, v)
        return jnp.einsum('bhid,hdm->bim', o, wo)

    def _L0_ffn_ref(x, Wqkv, q_scale, k_scale, Wo, ln_g, ln_b, W1, b1, W2, b2):
        import jax, jax.numpy as jnp
        import numpy as np
        DIM = 128
        DEPTH = 6
        HEADS = 16
        DIM_HEAD = 64
        WINDOW = 32
        INNER = HEADS * DIM_HEAD
        DIM_INNER = int(DIM * 4 * 2 / 3)
        QK_SCALE = 8.0

        def shift_tokens(t):
            a, s = jnp.split(t, 2, -1)
            s = jnp.pad(s, ((0, 0), (1, 0), (0, 0)))[:, :-1]
            return jnp.concatenate([a, s], -1)

        def l2norm(t):
            return t / jnp.maximum(jnp.linalg.norm(t, axis=-1, keepdims=True), 1e-12)

        def rotate_half(x):
            x1, x2 = jnp.split(x, 2, -1)
            return jnp.concatenate([-x2, x1], -1)

        def rotary_tables(n):
            half = jnp.arange(0, DIM_HEAD, 2, dtype=jnp.float32)
            inv_freq = 1.0 / 10000.0 ** (half / DIM_HEAD)
            t = jnp.arange(n, dtype=jnp.float32)
            freqs = t[:, None] * inv_freq[None, :]
            freqs = jnp.concatenate([freqs, freqs], -1)
            base_scale = (half + 0.4 * DIM_HEAD) / (1.4 * DIM_HEAD)
            power = (t - n // 2) / (WINDOW // 2)
            scale = base_scale[None, :] ** power[:, None]
            scale = jnp.concatenate([scale, scale], -1)
            return (freqs, scale)

        def local_attention(q, k, v):
            b, h, n, d = q.shape
            w = WINDOW
            nw = n // w
            bq = q.reshape(b, h, nw, w, d)
            bk = k.reshape(b, h, nw, w, d)
            bv = v.reshape(b, h, nw, w, d)

            def look(t):
                p = jnp.pad(t, ((0, 0), (0, 0), (1, 0), (0, 0), (0, 0)))
                return jnp.concatenate([p[:, :, :nw], p[:, :, 1:]], axis=3)
            bk2, bv2 = (look(bk), look(bv))
            seq = jnp.arange(n).reshape(nw, w)
            seq_p = jnp.pad(seq, ((1, 0), (0, 0)), constant_values=-1)
            jt = jnp.concatenate([seq_p[:nw], seq_p[1:]], axis=1)
            it = seq[:, :, None]
            jb = jt[:, None, :]
            mask = (it < jb) | (it > jb + w) | (jb == -1)
            sim = jnp.einsum('bhwie,bhwje->bhwij', bq, bk2) * QK_SCALE
            sim = jnp.where(mask, -jnp.finfo(sim.dtype).max, sim)
            attn = jax.nn.softmax(sim, -1)
            out = jnp.einsum('bhwij,bhwje->bhwie', attn, bv2)
            return out.reshape(b, h, n, d)

        def attn_layer(x, Wqkv, qs, ksc, Wo):
            b, n, _ = x.shape
            qkv = x @ Wqkv
            q, k, v = jnp.split(qkv, 3, -1)
            sh = lambda t: t.reshape(b, n, HEADS, DIM_HEAD).transpose(0, 2, 1, 3)
            q, k, v = (sh(q), sh(k), sh(v))
            q = l2norm(q) * qs
            k = l2norm(k) * ksc
            freqs, scale = rotary_tables(n)
            cos, sin = (jnp.cos(freqs), jnp.sin(freqs))
            q = q * cos * scale + rotate_half(q) * sin * scale
            inv = 1.0 / scale
            k = k * cos * inv + rotate_half(k) * sin * inv
            out = local_attention(q, k, v)
            out = out.transpose(0, 2, 1, 3).reshape(b, n, INNER)
            return out @ Wo

        def ffn_layer(x, g, bln, W1, b1, W2, b2):
            mu = x.mean(-1, keepdims=True)
            var = ((x - mu) ** 2).mean(-1, keepdims=True)
            xn = (x - mu) / jnp.sqrt(var + 1e-05) * g + bln
            hg = xn @ W1 + b1
            a, gate = jnp.split(hg, 2, -1)
            return a * jax.nn.gelu(gate, approximate=False) @ W2 + b2
        for i in range(DEPTH):
            x = attn_layer(shift_tokens(x), Wqkv[i], q_scale[i], k_scale[i], Wo[i]) + x
            x = ffn_layer(shift_tokens(x), ln_g[i], ln_b[i], W1[i], b1[i], W2[i], b2[i]) + x
        return x
    x = L0_attn_x
    mod = (_silu(L0_c) @ L0_wmod).reshape(L0_c.shape[0], 6, 1, -1)
    sa, ca, ga, sb, cb, gb = (mod[:, 0], mod[:, 1], mod[:, 2], mod[:, 3], mod[:, 4], mod[:, 5])
    ga = (2 * (ga >= 0) - 1) * jnp.maximum(jnp.abs(ga), 0.25)
    gb = (2 * (gb >= 0) - 1) * jnp.maximum(jnp.abs(gb), 0.25)
    h = _layernorm(x, axis=-1) * (1 + ca) + sa
    x = x + ga * _L0_attn_ref(h, L0_attn_wq, L0_attn_wk, L0_attn_wv, L0_attn_wo)
    h = _layernorm(x, axis=-1) * (1 + cb) + sb
    x = x + gb * _L0_ffn_ref(h, L0_ffn_Wqkv, L0_ffn_q_scale, L0_ffn_k_scale, L0_ffn_Wo, L0_ffn_ln_g, L0_ffn_ln_b, L0_ffn_W1, L0_ffn_b1, L0_ffn_W2, L0_ffn_b2)
    return x

_drawn_inputs = setup_inputs


def setup_inputs(seed=0):
    import zlib

    import numpy as np

    out = dict(_drawn_inputs(seed))
    spreads = {'L0_ffn_q_scale': (1.0, 0.6),
     'L0_ffn_k_scale': (1.0, 0.6),
     'L0_ffn_ln_g': (1.0, 0.6),
     'L0_ffn_ln_b': (0.0, 0.8),
     'L0_ffn_b1': (0.0, 0.8),
     'L0_ffn_b2': (0.0, 0.662)}
    factors = {'L0_attn_wq': 6.164, 'L0_attn_wk': 6.152, 'L0_ffn_W1': 7.452, 'L0_ffn_W2': 7.314}
    for name, (base, spread) in spreads.items():
        noise = np.random.default_rng([zlib.crc32(name.encode()), seed]).standard_normal(out[name].shape)
        drawn = base * np.exp(spread * noise) if base else spread * noise
        out[name] = jnp.asarray(drawn.astype(out[name].dtype))
    for name, factor in factors.items():
        out[name] = (out[name] * factor).astype(out[name].dtype)
    return out
```

```python
from contextlib import ExitStack

import numpy as np

import concourse.bass as bass
from concourse import mybir

F32 = mybir.dt.float32
BF16 = mybir.dt.bfloat16
ACT = mybir.ActivationFunctionType
ALU = mybir.AluOpType
AX = mybir.AxisListType

P = 128
B, T, M = 8, 256, 128
NT = T // P
CH = 512
INNER = 1024
GROUPS = INNER // CH
DEPTH, HB, DB, WIN = 6, 16, 64, 32
NW = T // WIN
HA, DA = 8, 128
F = int(M * 4 * 2 / 3)
NEG = -1.0e30
QK = GROUPS * NT * 2
NCH = GROUPS * NT * 3
UNITS = 4
PAIRS = HB // 2
EPS = 1e-5
NEWTON = 3
RSQRT = 3 + 3 * NEWTON
I32 = mybir.dt.int32


class Ev:

    def __init__(self, sem, per, credit=0, step=1):
        self.sem, self.per, self.credit, self.step = sem, per, credit, step

    def value(self, it, k):
        return it * (self.per * self.step) + (self.credit + (k + 1) * self.step)


def done(eng, ev, it, k=0):
    v = ev.value(it, k)
    if isinstance(v, int) and v <= ev.credit:
        return
    eng.wait_ge(ev.sem, v)


def settle(eng, ev):
    eng.sem_inc(ev.sem, 1)


def free(eng, ev, it, k, ring):
    done(eng, ev, it, k - ring)


def build(nc, x, wq, wk, wv, wo, Wqkv, q_scale, k_scale, Wo, ln_g, ln_b, W1, b1, W2, b2, c, wmod,
          ident_in, masks_in, ropeA_in, ropeB_in, out):
    with ExitStack() as ctx:
        def sb(name, shape, dt=F32):
            return ctx.enter_context(nc.sbuf_tensor(name, shape, dt))

        def ev(name, per, credit=0, step=1):
            e = Ev(ctx.enter_context(nc.semaphore(name)), per, credit, step)
            events.append(e)
            return e

        events = []
        ident = sb("ident", [P, P])
        ident16 = sb("ident16", [P, P], BF16)
        mask_f = sb("mask_f", [P, 2, CH])
        maskA = sb("maskA", [P, 3 * P], BF16)
        maskB = sb("maskB", [P, CH], BF16)
        ones = sb("ones", [1, P])
        ropeA = sb("ropeA", [P, NT, 2, DA])
        ropeB = sb("ropeB", [P, NT, 4, DB])
        rope = sb("rope", [P, NT, 4, DB])
        qks = sb("qks", [P, 4, DB])
        wqkvA = sb("wqkvA", [P, 3, INNER])
        woA = sb("woA", [P, HA, M])
        wqkvB = sb("wqkvB", [P, 3, INNER])
        woB = sb("woB", [P, PAIRS, M])
        w1 = sb("w1", [P, 2 * F])
        w2 = sb("w2", [P, 3, M])
        b1r = sb("b1r", [1, 2 * F])
        b2r = sb("b2r", [1, M])
        lng = sb("lng", [P, 1])
        lnb = sb("lnb", [P, 1])
        x0 = sb("x0", [P, B * NT, M])
        x1 = sb("x1", [P, B * NT, M])
        xr = sb("xr", [P, B * NT, M])
        gb = sb("gb", [P, B, M])
        wm = sb("wm", [P, 6 * M])
        cr = sb("cr", [B, M])
        cT = sb("cT", [P, 4, B])
        cb = sb("cb", [P, P])
        mod = sb("mod", [P, 6, M])
        gate = sb("gate", [P, 2, M])
        ga = sb("ga", [P, 2, M])
        stat = sb("stat", [P, NT, 6])
        mv = sb("mv", [P, NT, 2])
        rstd = sb("rstd", [P, NT])
        var = sb("var", [P, NT])
        nt = sb("nt", [P, 2, 32])
        ln = sb("ln", [P, NT, M])
        hm = sb("hm", [P, NT, M])
        xcur = sb("xcur", [P, NT, M])
        hT = sb("hT", [P, T])
        xsT = sb("xsT", [P, T])
        raw = sb("raw", [P, 2, CH])
        sq = sb("sq", [P, 2, CH])
        ra = sb("ra", [P, 4, CH])
        rb = sb("rb", [P, 2, CH])
        qn = sb("qn", [P, 4, CH])
        ss = sb("ss", [P, 4, 8])
        rs = sb("rs", [P, 4, 8])
        v = [sb(f"v{g}", [P, NT, CH]) for g in range(GROUPS)]
        vs = [sb(f"vs{g}", [P, NT, CH]) for g in range(GROUPS)]
        qT = [sb(f"qT{g}", [P, 4, T]) for g in range(GROUPS)]
        qd = [sb(f"qd{g}", [P, 4, NW, 2 * WIN]) for g in range(GROUPS)]
        kT = [sb(f"kT{g}", [P, 4, WIN + T]) for g in range(GROUPS)]
        dif = sb("dif", [P, 2, CH])
        pr = sb("pr", [P, 2, CH])
        mx = sb("mx", [P, 2, 8])
        sm = sb("sm", [P, 2, 8])
        rl = sb("rl", [P, 2, 8])
        pt = sb("pt", [P, 2, 4, 2, 2, 2 * WIN])
        ptA = sb("ptA", [P, 2, 3 * P])
        oT = sb("oT", [P, PAIRS, T])
        xnT = sb("xnT", [P, T])
        gel = sb("gel", [P, F])
        gg = sb("gg", [P, F])
        ggT = sb("ggT", [P, 3, P])
        yo = sb("yo", [P, NT, M])

        def bank(name):
            return ctx.enter_context(nc.psum_tensor(name, [P, CH], F32))

        pQ = [bank("pQ0"), bank("pQ1")]
        pT = bank("pT")
        pS = [bank("pS0"), bank("pS1")]
        pP = bank("pP")
        pO = bank("pO")
        pM = bank("pM")

        e_const = ev("e_const", 1, step=16 * 11)
        e_set = ev("e_set", 1)
        e_hold = ev("e_hold", 1)
        e_bar = ev("e_bar", 1)
        a_cT = ev("a_cT", 1)
        a_e = ev("a_e", 1)
        a_si = ev("a_si", 3)
        a_cb = ev("a_cb", 1)
        a_mo = ev("a_mo", 1)
        a_mc = ev("a_mc", 1)
        a_g = ev("a_g", 5)
        a_st = ev("a_st", 4)
        a_h = ev("a_h", 3)
        a_hT = ev("a_hT", 1)
        a_hc = ev("a_hc", 1)
        a_pj = ev("a_pj", NCH, NCH)
        a_ev = ev("a_ev", NCH, 2)
        a_ab = ev("a_ab", QK, 2)
        a_qn = ev("a_qn", QK, 2)
        a_tr = ev("a_tr", QK, 4)
        a_tc = ev("a_tc", QK, 1)
        a_S = ev("a_S", HA, HA)
        a_mx = ev("a_mx", HA)
        a_nm = ev("a_nm", HA)
        a_ex = ev("a_ex", HA, 2)
        a_rl = ev("a_rl", HA)
        a_pn = ev("a_pn", HA)
        a_pt = ev("a_pt", HA, 2)
        a_pc = ev("a_pc", HA, 1)
        a_pv = ev("a_pv", HA, HA)
        a_oc = ev("a_oc", HA, 1)
        a_wo = ev("a_wo", 1, 1)
        a_y = ev("a_y", 2)
        a_s2 = ev("a_s2", 4)
        a_str = ev("a_str", RSQRT)
        a_s2r = ev("a_s2r", RSQRT)
        a_x = ev("a_x", 2)
        e_wq = ev("e_wq", 1, step=16 * 8)
        e_w1 = ev("e_w1", 1, step=16 * 8)
        b_rp = ev("b_rp", 1)
        b_xc = ev("b_xc", 1)
        b_xt = ev("b_xt", 1, 1)
        b_xs = ev("b_xs", 1)
        b_pj = ev("b_pj", NCH, NCH)
        b_ev = ev("b_ev", NCH, 2)
        b_ss = ev("b_ss", QK)
        b_mxs = ev("b_mxs", GROUPS)
        b_rs = ev("b_rs", GROUPS * RSQRT)
        b_ab = ev("b_ab", QK, 2)
        b_ad = ev("b_ad", QK, 2)
        b_qn = ev("b_qn", QK)
        b_tr = ev("b_tr", QK, 4)
        b_tc = ev("b_tc", QK, 1)
        b_vs = [ev(f"b_vs{g}", 1, step=16 * 2) for g in range(GROUPS)]
        b_S = ev("b_S", UNITS, UNITS)
        b_mx = ev("b_mx", UNITS)
        b_sub = ev("b_sub", UNITS, 2)
        b_ex = ev("b_ex", UNITS, 2)
        b_sm = ev("b_sm", UNITS)
        b_rl = ev("b_rl", UNITS)
        b_pn = ev("b_pn", UNITS)
        b_pt = ev("b_pt", UNITS, 2)
        b_pc = ev("b_pc", UNITS, 1)
        b_pv = ev("b_pv", PAIRS, PAIRS)
        b_oc = ev("b_oc", PAIRS, 1)
        b_wo = ev("b_wo", 1, 1)
        b_wx = ev("b_wx", 1, 2)
        f_xc = ev("f_xc", 1)
        f_x1 = ev("f_x1", 1, 1)
        f_c1 = ev("f_c1", 1)
        f_x2 = ev("f_x2", 1)
        f_st = ev("f_st", 3)
        f_str = ev("f_str", RSQRT)
        f_xn = ev("f_xn", 1)
        f_x3 = ev("f_x3", 1)
        f_xg = ev("f_xg", 1)
        f_h = ev("f_h", NT)
        f_ge = ev("f_ge", NT)
        f_G = ev("f_G", NT, 1)
        f_gt = ev("f_gt", NT)
        f_gc = ev("f_gc", NT)
        f_y = ev("f_y", NT)
        f_x = ev("f_x", NT, 1)
        o_m = ev("o_m", 3)
        o_out = ev("o_out", 1, step=16)

        block = ctx.enter_context(nc.Block())

        def barrier(eng, n):
            eng.drain().then_inc(e_bar.sem, 1)
            eng.wait_ge(e_bar.sem, (n + 1) * 4)
            settle(eng, e_hold)

        def rsqrt(e, evt, it, n, y, x_, h, t):
            k = [n * RSQRT]

            def then(i):
                i.then_inc(evt.sem, 1)
                done(e, evt, it, k[0])
                k[0] += 1

            then(e.tensor_scalar(t.bitcast(I32), x_.bitcast(I32), 1, None, ALU.arith_shift_right))
            then(e.tensor_scalar(y.bitcast(I32), t.bitcast(I32), -1.0, float(0x5F3759DF), ALU.mult, ALU.add))
            then(e.tensor_scalar(h, x_, -0.5, None, ALU.mult))
            for _ in range(NEWTON):
                then(e.tensor_tensor(t, y, y, ALU.mult))
                then(e.tensor_tensor(t, t, h, ALU.mult))
                then(e.scalar_tensor_tensor(y, t, 1.5, y, ALU.add, ALU.mult))

        def chunk(c):
            return c // 6, (c % 6) // 3, c % 3

        def a_front(en, e, b):
            if en == "dve":
                done(e, a_si, 0, 2)
                if not (isinstance(b, int) and b == 0):
                    done(e, a_mo, b - 1)
                e.tensor_copy(cb[:, :], cT[:, 3, bass.ds(b, 1)].to_broadcast([P, P])).then_inc(a_cb.sem, 1)
                xin = x0[:, bass.ds(b * NT, NT), :]
                settle(e, e_hold)
                for t in range(NT):
                    i = e.bn_stats(stat[:, t, :], xin[:, t, :])
                i.then_inc(a_st.sem, 1)
                done(e, a_st, b, 0)
                settle(e, e_hold)
                for t in range(NT):
                    i = e.bn_aggr(mv[:, t, :], stat[:, t, :])
                i.then_inc(a_st.sem, 1)
                done(e, a_st, b, 1)
                e.tensor_scalar(var[:, :], mv[:, :, 1], EPS, None, ALU.add).then_inc(a_st.sem, 1)
                done(e, a_st, b, 2)
                rsqrt(e, a_str, b, 0, rstd[:, :], var[:, :], nt[:, 0, 0:NT], nt[:, 1, 0:NT])
                for t in range(NT):
                    i = e.tensor_scalar(ln[:, t, :], xin[:, t, :], mv[:, t, 0:1], rstd[:, t:t + 1],
                                        ALU.subtract, ALU.mult)
                i.then_inc(a_st.sem, 1)
                done(e, a_mc, b)
                g3 = mod[:, 2::3, :]
                e.tensor_scalar(gate[:, :, :], g3, 0.0, 2.0, ALU.is_ge, ALU.mult).then_inc(a_g.sem, 1)
                done(e, a_g, b, 0)
                e.tensor_scalar(gate[:, :, :], gate[:, :, :], -1.0, None, ALU.add).then_inc(a_g.sem, 1)
                e.scalar_tensor_tensor(ga[:, :, :], g3, -1.0, g3, ALU.mult, ALU.max).then_inc(a_g.sem, 1)
                e.tensor_scalar(mod[:, 1::3, :], mod[:, 1::3, :], 1.0, None, ALU.add).then_inc(a_g.sem, 1)
                done(e, a_g, b, 3)
                e.scalar_tensor_tensor(gate[:, :, :], ga[:, :, :], 0.25, gate[:, :, :], ALU.max, ALU.mult)\
                 .then_inc(a_g.sem, 1)
                done(e, a_st, b, 3)
                e.tensor_tensor(ln[:, :, :], ln[:, :, :], mod[:, 1:2, :].to_broadcast([P, NT, M]),
                                ALU.mult).then_inc(a_h.sem, 1)
                done(e, a_h, b, 0)
                e.tensor_tensor(hm[:, :, :], ln[:, :, :], mod[:, 0:1, :].to_broadcast([P, NT, M]),
                                ALU.add).then_inc(a_h.sem, 1)
                done(e, a_g, b, 4)
                e.tensor_copy(gb[:, bass.ds(b, 1), :], gate[:, 1:2, :]).then_inc(a_h.sem, 1)
            if en == "pe":
                done(e, a_cb, b)
                free(e, a_ev, b, 1, 2)
                for n in range(2):
                    i = e.matmul(pQ[n][:, 0:3 * M], cb[:, :], wm[:, n * 3 * M:(n + 1) * 3 * M],
                                 start=True, stop=True)
                i.then_inc(a_mo.sem, 1)
                done(e, a_h, b, 1)
                for t in range(NT):
                    i = e.transpose(pM[:, t * M:(t + 1) * M], hm[:, t, :], ident[:, :])
                i.then_inc(a_hT.sem, 1)
            if en == "act":
                done(e, a_mo, b)
                if not (isinstance(b, int) and b == 0):
                    done(e, a_x, b - 1, 1)
                for n in range(2):
                    i = e.copy(mod[:, 3 * n:3 * n + 3, :], pQ[n][:, 0:3 * M])
                i.then_inc(a_mc.sem, 1)
                done(e, a_hT, b)
                free(e, a_pj, b, 11, NCH)
                e.copy(hT[:, :], pM[:, 0:T]).then_inc(a_hc.sem, 1)

        def a_chunk(en, e, b, c_):
            g, t, kind = chunk(c_)
            j = g * 4 + t * 2 + kind
            if en == "pe":
                if c_ == 0:
                    done(e, a_hc, b)
                    done(e, a_mc, b)
                free(e, a_ev, b, c_, 2)
                e.matmul(pQ[c_ % 2][:, :], hT[:, t * P:(t + 1) * P], wqkvA[:, kind, g * CH:(g + 1) * CH],
                         start=True, stop=True).then_inc(a_pj.sem, 1)
            if en == "act":
                done(e, a_pj, b, c_)
                if kind == 2:
                    free(e, a_pv, b, 4 * g + 3, HA)
                    e.copy(v[g][:, t, :], pQ[c_ % 2][:, :]).then_inc(a_ev.sem, 1)
                else:
                    free(e, a_ab, b, j, 2)
                    e.copy(raw[:, j % 2, :], pQ[c_ % 2][:, :]).then_inc(a_ev.sem, 1)
            if en == "dve" and kind < 2:
                done(e, a_ev, b, c_)
                r = raw[:, j % 2, :].rearrange("p (h s d) -> p h s d", s=2, d=DA // 2)
                shape = [P, 4, 2, DA // 2]
                cos, sin = (ropeA[:, t:t + 1, n, :].rearrange("p o (s d) -> p o s d", s=2).to_broadcast(shape)
                            for n in range(2))
                free(e, a_qn, b, j, 2)
                oa, ob = (y[:, j % 2, :].rearrange("p (h s d) -> p h s d", s=2, d=DA // 2) for y in (ra, rb))
                e.tensor_tensor(oa, r, cos, ALU.mult)
                e.tensor_tensor(ob, r[:, :, ::-1, :], sin, ALU.mult).then_inc(a_ab.sem, 1)
            if en == "pool" and kind < 2:
                done(e, a_ab, b, j)
                free(e, a_tr, b, j, 4)
                e.tensor_tensor(qn[:, j % 4, :], ra[:, j % 2, :], rb[:, j % 2, :], ALU.add).then_inc(a_qn.sem, 1)

        def a_turn(en, e, b, j):
            g, t, isk = j // 4, (j % 4) // 2, j % 2
            if en == "pe":
                done(e, a_qn, b, j)
                free(e, a_tc, b, j, 1)
                for h in range(4):
                    i = e.transpose(pT[:, h * P:(h + 1) * P], qn[:, j % 4, h * P:(h + 1) * P], ident[:, :])
                i.then_inc(a_tr.sem, 1)
            if en == "act":
                done(e, a_tr, b, j)
                free(e, a_S, b, 4 * g + 3, HA)
                dst = kT[g][:, :, WIN + t * P:WIN + (t + 1) * P] if isk else qT[g][:, :, t * P:(t + 1) * P]
                e.copy(dst, pT[:, :].rearrange("p (h q) -> p h q", h=4)).then_inc(a_tc.sem, 1)

        def a_scores(en, e, b, h):
            g, s = h // 4, h % 2
            rows = ((0, P), (P, 3 * P))
            if en == "pe":
                done(e, a_tc, b, 4 * g + 3)
                free(e, a_ex, b, h, 2)
                e.matmul(pS[s][:, 0:3 * P], ident16[:, :], maskA[:, :], start=True, stop=False,
                         skip_group_check=True)
                for t, (lo, hi) in enumerate(rows):
                    i = e.matmul(pS[s][:, lo:hi], qT[g][:, h % 4, t * P:(t + 1) * P],
                                 kT[g][:, h % 4, WIN:WIN + (t + 1) * P], start=False, stop=True,
                                 skip_group_check=True)
                i.then_inc(a_S.sem, 1)
            if en == "dve":
                done(e, a_S, b, h)
                for t, (lo, hi) in enumerate(rows):
                    i = e.tensor_reduce(mx[:, s, t:t + 1], pS[s][:, lo:hi], AX.X, ALU.max)
                i.then_inc(a_mx.sem, 1)
                done(e, a_mx, b, h)
                e.tensor_scalar(mx[:, s, 2:4], mx[:, s, 0:2], -1.0 / DA, None, ALU.mult).then_inc(a_nm.sem, 1)
            if en == "act":
                done(e, a_nm, b, h)
                free(e, a_pt, b, h, 2)
                for t, (lo, hi) in enumerate(rows):
                    i = e.activation(pr[:, s, lo:hi], pS[s][:, lo:hi], ACT.Exp, bias=mx[:, s, 2 + t:3 + t],
                                     scale=1.0 / DA, accum_out=sm[:, s, t:t + 1])
                i.then_inc(a_ex.sem, 1)

        def a_norm(en, e, b, h):
            s = h % 2
            if en == "dve":
                done(e, a_ex, b, h)
                e.reciprocal(rl[:, s, 0:2], sm[:, s, 0:2]).then_inc(a_rl.sem, 1)
                done(e, a_rl, b, h)
                for t, (lo, hi) in enumerate(((0, P), (P, 3 * P))):
                    i = e.tensor_scalar(pr[:, s, lo:hi], pr[:, s, lo:hi], rl[:, s, t:t + 1], None, ALU.mult)
                i.then_inc(a_pn.sem, 1)

        def a_values(en, e, b, h):
            g, s = h // 4, h % 2
            if en == "pe":
                done(e, a_pn, b, h)
                free(e, a_pc, b, h, 1)
                for n in range(3):
                    i = e.transpose(pP[:, n * P:(n + 1) * P], pr[:, s, n * P:(n + 1) * P], ident[:, :])
                i.then_inc(a_pt.sem, 1)
                done(e, a_pc, b, h)
                done(e, a_ev, b, g * 6 + 5)
                free(e, a_oc, b, h, 1)
                for n, (q, k) in enumerate(((0, 0), (1, 0), (1, 1))):
                    i = e.matmul(pO[:, q * P:(q + 1) * P], v[g][:, k, (h % 4) * P:(h % 4 + 1) * P],
                                 ptA[:, s, n * P:(n + 1) * P], start=(k == 0), stop=(k == q))
                i.then_inc(a_pv.sem, 1)
            if en == "act":
                done(e, a_pt, b, h)
                free(e, a_pv, b, h, 2)
                e.copy(ptA[:, s, :], pP[:, 0:3 * P]).then_inc(a_pc.sem, 1)
                done(e, a_pv, b, h)
                if h == 0:
                    free(e, a_wo, b, 0, 1)
                e.copy(oT[:, h, :], pO[:, 0:T]).then_inc(a_oc.sem, 1)

        def a_out(en, e, b):
            if en == "pe":
                done(e, a_oc, b, HA - 1)
                done(e, a_hc, b)
                for t in range(NT):
                    for h in range(HA):
                        i = e.matmul(pM[:, t * M:(t + 1) * M], oT[:, h, t * P:(t + 1) * P], woA[:, h, :],
                                     start=(h == 0), stop=(h == HA - 1))
                i.then_inc(a_wo.sem, 1)
            if en == "dve":
                done(e, a_wo, b)
                xi, xo = x0[:, bass.ds(b * NT, NT), :], x1[:, bass.ds(b * NT, NT), :]
                e.tensor_tensor(yo[:, :, :], pM[:, 0:T].rearrange("p (t m) -> p t m", t=NT),
                                gate[:, 0:1, :].to_broadcast([P, NT, M]), ALU.mult).then_inc(a_y.sem, 1)
                done(e, a_y, b, 0)
                e.tensor_tensor(xo, xi, yo[:, :, :], ALU.add).then_inc(a_y.sem, 1)
                done(e, a_y, b, 1)
                settle(e, e_hold)
                for t in range(NT):
                    i = e.bn_stats(stat[:, t, :], xo[:, t, :])
                i.then_inc(a_s2.sem, 1)
                done(e, a_s2, b, 0)
                settle(e, e_hold)
                for t in range(NT):
                    i = e.bn_aggr(mv[:, t, :], stat[:, t, :])
                i.then_inc(a_s2.sem, 1)
                done(e, a_s2, b, 1)
                e.tensor_scalar(var[:, :], mv[:, :, 1], EPS, None, ALU.add).then_inc(a_s2.sem, 1)
                done(e, a_s2, b, 2)
                rsqrt(e, a_s2r, b, 0, rstd[:, :], var[:, :], nt[:, 0, 0:NT], nt[:, 1, 0:NT])
                for t in range(NT):
                    i = e.tensor_scalar(ln[:, t, :], xo[:, t, :], mv[:, t, 0:1], rstd[:, t:t + 1],
                                        ALU.subtract, ALU.mult)
                i.then_inc(a_s2.sem, 1)
                done(e, a_s2, b, 3)
                e.tensor_tensor(ln[:, :, :], ln[:, :, :], mod[:, 4:5, :].to_broadcast([P, NT, M]),
                                ALU.mult).then_inc(a_x.sem, 1)
                done(e, a_x, b, 0)
                e.tensor_tensor(xr[:, bass.ds(b * NT, NT), :], ln[:, :, :],
                                mod[:, 3:4, :].to_broadcast([P, NT, M]), ALU.add).then_inc(a_x.sem, 1)

        def a_pass(en, e, b):
            a_front(en, e, b)
            for c_ in range(6):
                a_chunk(en, e, b, c_)
            for j in range(4):
                a_turn(en, e, b, j)
            for c_ in range(6, 12):
                a_chunk(en, e, b, c_)
                if c_ < 10:
                    a_scores(en, e, b, c_ - 6)
                if 7 <= c_ < 11:
                    a_norm(en, e, b, c_ - 7)
                if c_ >= 8:
                    a_values(en, e, b, c_ - 8)
            for j in range(4, 8):
                a_turn(en, e, b, j)
            for h in range(4, 10):
                if h < 8:
                    a_scores(en, e, b, h)
                if 5 <= h < 9:
                    a_norm(en, e, b, h - 1)
                if h >= 6:
                    a_values(en, e, b, h - 2)
            a_out(en, e, b)

        def turn_in(en, e, it, b):
            if en == "pool":
                free(e, b_xt, it, 0, 1)
                settle(e, e_hold)
                e.tensor_copy(xcur[:, :, :], xr[:, bass.ds(b * NT, NT), :]).then_inc(b_xc.sem, 1)
            if en == "pe":
                done(e, b_xc, it)
                free(e, b_wx, it, 0, 2)
                for t in range(NT):
                    i = e.transpose(pM[:, t * M:(t + 1) * M], xcur[:, t, :], ident[:, :])
                i.then_inc(b_xt.sem, 1)
            if en == "act":
                done(e, b_xt, it)
                free(e, b_pj, it, NCH - 1, NCH)
                e.copy(xsT[0:64, :], pM[0:64, 0:T])
                e.copy(xsT[64:P, 1:T], pM[64:P, 0:T - 1]).then_inc(b_xs.sem, 1)

        def project(en, e, it, c_):
            g, t, kind = chunk(c_)
            j = g * 4 + t * 2 + kind
            if en == "pe":
                if c_ == 0:
                    done(e, b_xs, it)
                free(e, b_ev, it, c_, 2)
                e.matmul(pQ[c_ % 2][:, :], xsT[:, t * P:(t + 1) * P], wqkvB[:, kind, g * CH:(g + 1) * CH],
                         start=True, stop=True).then_inc(b_pj.sem, 1)
            if en == "act":
                done(e, b_pj, it, c_)
                if kind == 2:
                    free(e, b_pv, it, 4 * g + 3, PAIRS)
                    e.copy(v[g][:, t, :], pQ[c_ % 2][:, :]).then_inc(b_ev.sem, 1)
                else:
                    free(e, b_ab, it, j, 2)
                    e.copy(raw[:, j % 2, :], pQ[c_ % 2][:, :])
                    e.activation(sq[:, j % 2, :], pQ[c_ % 2][:, :], ACT.Square).then_inc(b_ev.sem, 1)
            if en == "dve" and kind < 2:
                done(e, b_ev, it, c_)
                free(e, b_ad, it, j, 2)
                e.tensor_reduce(ss[:, j % 4, :], sq[:, j % 2, :].rearrange("p (h d) -> p h d", d=DB),
                                AX.X, ALU.add).then_inc(b_ss.sem, 1)
                r = raw[:, j % 2, :].rearrange("p (h s d) -> p h s d", s=2, d=DB // 2)
                shape = [P, 8, 2, DB // 2]
                cos, sin = (rope[:, t:t + 1, 2 * kind + n, :].rearrange("p o (s d) -> p o s d", s=2)
                            .to_broadcast(shape) for n in range(2))
                oa, ob = (y.rearrange("p (h s d) -> p h s d", s=2, d=DB // 2)
                          for y in (ra[:, j % 4, :], rb[:, j % 2, :]))
                e.tensor_tensor(oa, r, cos, ALU.mult)
                e.tensor_tensor(ob, r[:, :, ::-1, :], sin, ALU.mult).then_inc(b_ab.sem, 1)
            if en == "pool" and kind < 2:
                done(e, b_ab, it, j)
                e.tensor_tensor(ra[:, j % 4, :], ra[:, j % 4, :], rb[:, j % 2, :], ALU.add).then_inc(b_ad.sem, 1)

        def norms(en, e, it, g):
            if en == "dve":
                done(e, b_ss, it, 4 * g + 3)
                e.tensor_scalar(ss[:, :, :], ss[:, :, :], 1e-24, None, ALU.max).then_inc(b_mxs.sem, 1)
                done(e, b_mxs, it, g)
                flat = lambda y: y.rearrange("p n h -> p (n h)")
                rsqrt(e, b_rs, it, g, flat(rs[:, :, :]), flat(ss[:, :, :]), nt[:, 0, :], nt[:, 1, :])

        def normalise(en, e, it, j):
            if en == "dve":
                done(e, b_ad, it, j)
                free(e, b_tr, it, j, 4)
                e.tensor_tensor(qn[:, j % 4, :].rearrange("p (h d) -> p h d", d=DB),
                                ra[:, j % 4, :].rearrange("p (h d) -> p h d", d=DB),
                                rs[:, j % 4, :].unsqueeze(2).to_broadcast([P, 8, DB]), ALU.mult)\
                 .then_inc(b_qn.sem, 1)

        def turn(en, e, it, j):
            g, t, isk = j // 4, (j % 4) // 2, j % 2
            if en == "pe":
                done(e, b_qn, it, j)
                free(e, b_tc, it, j, 1)
                for p in range(4):
                    i = e.transpose(pT[:, p * P:(p + 1) * P], qn[:, j % 4, p * P:(p + 1) * P], ident[:, :])
                i.then_inc(b_tr.sem, 1)
            if en == "act":
                done(e, b_tr, it, j)
                free(e, b_S, it, 2 * g + 1, UNITS)
                if isk:
                    e.copy(kT[g][:, :, WIN + t * P:WIN + (t + 1) * P],
                           pT[:, :].rearrange("p (h q) -> p h q", h=4)).then_inc(b_tc.sem, 1)
                else:
                    for s in range(2):
                        i = e.copy(qd[g][64 * s:64 * s + 64, :, 4 * t:4 * t + 4, WIN * s:WIN * s + WIN],
                                   pT[64 * s:64 * s + 64, :].rearrange("p (h w q) -> p h w q", h=4, w=4))
                    i.then_inc(b_tc.sem, 1)

        def scores(en, e, it, u):
            g, s = u // 2, u % 2
            if en == "pe":
                done(e, b_tc, it, 4 * g + 3)
                free(e, b_sub, it, u, 2)
                e.matmul(pS[s][:, :], ident16[:, :], maskB[:, :], start=True, stop=False, skip_group_check=True)
                for p2 in range(2):
                    for w in range(NW):
                        lo = p2 * 256 + (w // 2) * 64
                        i = e.matmul(pS[s][64 * (w % 2):64 * (w % 2) + 64, lo:lo + 64],
                                     qd[g][:, 2 * (u % 2) + p2, w, :],
                                     kT[g][:, 2 * (u % 2) + p2, WIN * w:WIN * w + 2 * WIN],
                                     start=False, stop=True, skip_group_check=True)
                i.then_inc(b_S.sem, 1)
            if en == "dve":
                done(e, b_S, it, u)
                sc = pS[s][:, :].rearrange("p (n k) -> p n k", k=64)
                e.tensor_reduce(mx[:, s, :], sc, AX.X, ALU.max).then_inc(b_mx.sem, 1)
                done(e, b_mx, it, u)
                free(e, b_ex, it, u, 2)
                e.tensor_tensor(dif[:, s, :].rearrange("p (n k) -> p n k", k=64), sc,
                                mx[:, s, :].unsqueeze(2).to_broadcast([P, 8, 64]), ALU.subtract)\
                 .then_inc(b_sub.sem, 1)
            if en == "act":
                done(e, b_sub, it, u)
                free(e, b_pt, it, u, 2)
                e.activation(pr[:, s, :], dif[:, s, :], ACT.Exp, scale=8.0).then_inc(b_ex.sem, 1)

        def soft_norm(en, e, it, u):
            s = u % 2
            if en == "dve":
                done(e, b_ex, it, u)
                e.tensor_reduce(sm[:, s, :], pr[:, s, :].rearrange("p (n k) -> p n k", k=64),
                                AX.X, ALU.add).then_inc(b_sm.sem, 1)
                done(e, b_sm, it, u)
                e.reciprocal(rl[:, s, :], sm[:, s, :]).then_inc(b_rl.sem, 1)
            if en == "pool":
                done(e, b_rl, it, u)
                y = pr[:, s, :].rearrange("p (n k) -> p n k", k=64)
                e.tensor_tensor(y, y, rl[:, s, :].unsqueeze(2).to_broadcast([P, 8, 64]), ALU.mult)\
                 .then_inc(b_pn.sem, 1)

        def values(en, e, it, u):
            g, s = u // 2, u % 2
            if en == "pe":
                done(e, b_pn, it, u)
                free(e, b_pc, it, u, 1)
                for n in range(4):
                    i = e.transpose(pP[:, n * P:(n + 1) * P], pr[:, s, n * P:(n + 1) * P], ident[:, :])
                i.then_inc(b_pt.sem, 1)
                done(e, b_pc, it, u)
                done(e, b_ev, it, g * 6 + 5)
                done(e, b_vs[g], it)
            if en == "act":
                done(e, b_pt, it, u)
                free(e, b_pv, it, 2 * u + 1, 4)
                dst = pt[:, s, :, :, :, :].rearrange("p n a b k -> p (n a) b k")
                src = pP[:, :].rearrange("p (n k) -> p n k", k=64)
                for h in range(2):
                    i = e.copy(dst[64 * h:64 * h + 64, :, h, :], src[64 * h:64 * h + 64, :, :])
                i.then_inc(b_pc.sem, 1)
            for p2 in range(2):
                k, pair = 2 * u + p2, 2 * (u % 2) + p2
                if en == "pe":
                    free(e, b_oc, it, k, 1)
                    o = pO[:, :].rearrange("p (t a c q) -> p t a c q", t=NT, a=2, c=2)
                    for t in range(NT):
                        for par in range(2):
                            i = e.matmul(o[:, t, :, par, :], (v if par else vs)[g][:, t, pair * P:(pair + 1) * P],
                                         pt[:, s, 2 * p2 + t, par, :, :], start=(t == 0 and par == 0), stop=True,
                                         skip_group_check=True)
                    i.then_inc(b_pv.sem, 1)
                if en == "act":
                    done(e, b_pv, it, k)
                    if k == 0:
                        free(e, b_wo, it, 0, 1)
                    o = pO[:, :].rearrange("p (w h q) -> p w h q", h=2, q=WIN)
                    for h in range(2):
                        i = e.copy(oT[64 * h:64 * h + 64, k, :].rearrange("p (w q) -> p w q", q=WIN),
                                   o[64 * h:64 * h + 64, :, h, :])
                    i.then_inc(b_oc.sem, 1)

        def project_out(en, e, it, b, last):
            if en == "pe":
                done(e, b_oc, it, PAIRS - 1)
                done(e, b_xs, it if last else it + 1)
                for t in range(NT):
                    for k in range(PAIRS):
                        i = e.matmul(pM[:, t * M:(t + 1) * M], oT[:, k, t * P:(t + 1) * P], woB[:, k, :],
                                     start=(k == 0), stop=(k == PAIRS - 1))
                i.then_inc(b_wo.sem, 1)
            if en == "dve":
                done(e, b_wo, it)
                xd = xr[:, bass.ds(b * NT, NT), :]
                e.tensor_tensor(xd, pM[:, 0:T].rearrange("p (t m) -> p t m", t=NT), xd, ALU.add)\
                 .then_inc(b_wx.sem, 1)

        def move_values(e, it, g):
            done(e, b_ev, it, g * 6 + 5)
            settle(e, e_hold)
            free(e, b_pv, it, 4 * g + 3, PAIRS)
            settle(e, e_hold)
            e.dma_start(vs[g][WIN:P, :, :], v[g][0:P - WIN, :, :]).then_inc(b_vs[g].sem, 16)
            e.dma_start(vs[g][0:WIN, 1, :], v[g][P - WIN:P, 0, :]).then_inc(b_vs[g].sem, 16)

        def b_pass(en, e, l, b, first):
            it = l * B + b
            turn_in(en, e, it, b)
            for c_ in range(3):
                project(en, e, it, c_)
            if not first:
                values(en, e, it - 1, 2)
                soft_norm(en, e, it - 1, 3)
            for c_ in range(3, 6):
                project(en, e, it, c_)
            norms(en, e, it, 0)
            for j in range(4):
                normalise(en, e, it, j)
            if not first:
                values(en, e, it - 1, 3)
                project_out(en, e, it - 1, b - 1, False)
            for j in range(4):
                turn(en, e, it, j)
            project(en, e, it, 6)
            scores(en, e, it, 0)
            project(en, e, it, 7)
            soft_norm(en, e, it, 0)
            project(en, e, it, 8)
            scores(en, e, it, 1)
            project(en, e, it, 9)
            values(en, e, it, 0)
            soft_norm(en, e, it, 1)
            project(en, e, it, 10)
            project(en, e, it, 11)
            norms(en, e, it, 1)
            for j in range(4, 8):
                normalise(en, e, it, j)
            values(en, e, it, 1)
            for j in range(4, 8):
                turn(en, e, it, j)
            scores(en, e, it, 2)
            soft_norm(en, e, it, 2)
            scores(en, e, it, 3)

        def b_end(en, e, l):
            it = l * B + (B - 1)
            values(en, e, it, 2)
            soft_norm(en, e, it, 3)
            values(en, e, it, 3)
            project_out(en, e, it, B - 1, True)

        def f_pass(en, e, l, b):
            it = l * B + b
            xd = xr[:, bass.ds(b * NT, NT), :]
            if en == "pool":
                free(e, f_x1, it, 0, 1)
                settle(e, e_hold)
                e.tensor_copy(xcur[:, :, :], xd).then_inc(f_xc.sem, 1)
            if en == "pe":
                done(e, f_xc, it)
                for t in range(NT):
                    i = e.transpose(pM[:, t * M:(t + 1) * M], xcur[:, t, :], ident[:, :])
                i.then_inc(f_x1.sem, 1)
                done(e, f_c1, it)
                for t in range(NT):
                    i = e.transpose(pT[:, t * M:(t + 1) * M], xsT[:, t * P:(t + 1) * P], ident[:, :])
                i.then_inc(f_x2.sem, 1)
                done(e, f_xn, it)
                for t in range(NT):
                    i = e.transpose(pP[:, t * M:(t + 1) * M], ln[:, t, :], ident[:, :])
                i.then_inc(f_x3.sem, 1)
                done(e, f_xg, it)
            if en == "act":
                done(e, f_x1, it)
                e.copy(xsT[0:64, :], pM[0:64, 0:T])
                e.copy(xsT[64:P, 1:T], pM[64:P, 0:T - 1]).then_inc(f_c1.sem, 1)
            if en == "dve":
                done(e, f_x2, it)
                settle(e, e_hold)
                for t in range(NT):
                    i = e.bn_stats(stat[:, t, :], pT[:, t * M:(t + 1) * M])
                i.then_inc(f_st.sem, 1)
                done(e, f_st, it, 0)
                settle(e, e_hold)
                for t in range(NT):
                    i = e.bn_aggr(mv[:, t, :], stat[:, t, :])
                i.then_inc(f_st.sem, 1)
                done(e, f_st, it, 1)
                e.tensor_scalar(var[:, :], mv[:, :, 1], EPS, None, ALU.add).then_inc(f_st.sem, 1)
                done(e, f_st, it, 2)
                rsqrt(e, f_str, it, 0, rstd[:, :], var[:, :], nt[:, 0, 0:NT], nt[:, 1, 0:NT])
                for t in range(NT):
                    i = e.tensor_scalar(ln[:, t, :], pT[:, t * M:(t + 1) * M], mv[:, t, 0:1], rstd[:, t:t + 1],
                                        ALU.subtract, ALU.mult)
                i.then_inc(f_xn.sem, 1)
                done(e, f_x3, it)
                e.tensor_scalar(xnT[:, :], pP[:, 0:T], lng[:, 0:1], lnb[:, 0:1], ALU.mult, ALU.add)\
                 .then_inc(f_xg.sem, 1)
            for t in range(NT):
                sizes = (P, P, F - 2 * P)
                if en == "pe":
                    free(e, f_G, it, t, 1)
                    for n in range(2):
                        e.matmul(pQ[n][:, 0:F], ones[:, :], b1r[:, n * F:(n + 1) * F], start=True, stop=False)
                        i = e.matmul(pQ[n][:, 0:F], xnT[:, t * P:(t + 1) * P], w1[:, n * F:(n + 1) * F],
                                     start=False, stop=True)
                    i.then_inc(f_h.sem, 1)
                    done(e, f_G, it, t)
                    for n, k in enumerate(sizes):
                        i = e.transpose(pS[0][0:k, n * P:(n + 1) * P], gg[:, n * P:n * P + k], ident[:, :])
                    i.then_inc(f_gt.sem, 1)
                    done(e, f_gc, it, t)
                    free(e, f_x, it, t, 1)
                    e.matmul(pO[:, 0:M], ones[:, :], b2r[:, :], start=True, stop=False)
                    for n, k in enumerate(sizes):
                        i = e.matmul(pO[:, 0:M], ggT[0:k, n, :], w2[0:k, n, :], start=False, stop=(n == 2))
                    i.then_inc(f_y.sem, 1)
                if en == "act":
                    done(e, f_h, it, t)
                    e.activation(gel[:, :], pQ[1][:, 0:F], ACT.Gelu).then_inc(f_ge.sem, 1)
                    done(e, f_gt, it, t)
                    e.copy(ggT[:, 0:2, :], pS[0][:, 0:2 * P])
                    e.copy(ggT[0:sizes[2], 2, :], pS[0][0:sizes[2], 2 * P:3 * P]).then_inc(f_gc.sem, 1)
                if en == "dve":
                    done(e, f_ge, it, t)
                    e.tensor_tensor(gg[:, :], pQ[0][:, 0:F], gel[:, :], ALU.mult).then_inc(f_G.sem, 1)
                    done(e, f_y, it, t)
                    xt = xr[:, bass.ds(b * NT + t, 1), :]
                    e.tensor_tensor(xt, pO[:, 0:M].rearrange("p (o m) -> p o m", o=1), xt, ALU.add)\
                     .then_inc(f_x.sem, 1)

        def run(en, e):
            done(e, e_set, 0)
            if en == "pe":
                e.transpose(pM[:, 0:B], cr[:, :], ident[0:B, 0:B]).then_inc(a_cT.sem, 1)
            if en == "act":
                done(e, a_cT, 0)
                e.activation(cT[:, 1, :], pM[:, 0:B], ACT.Exp, scale=-1.0)
                e.copy(cT[:, 0, :], pM[:, 0:B]).then_inc(a_e.sem, 1)
            if en == "dve":
                done(e, a_e, 0)
                e.tensor_scalar(cT[:, 1, :], cT[:, 1, :], 1.0, None, ALU.add).then_inc(a_si.sem, 1)
                done(e, a_si, 0, 0)
                e.reciprocal(cT[:, 2, :], cT[:, 1, :]).then_inc(a_si.sem, 1)
                done(e, a_si, 0, 1)
                e.tensor_tensor(cT[:, 3, :], cT[:, 0, :], cT[:, 2, :], ALU.mult).then_inc(a_si.sem, 1)
            barrier(e, 0)
            with e.Fori(0, B) as b:
                a_pass(en, e, b)
            barrier(e, 1)
            with e.Fori(0, DEPTH) as l:
                done(e, e_wq, l)
                if en == "dve":
                    e.tensor_tensor(rope[:, :, :, :], ropeB[:, :, :, :],
                                    qks[:, :, :].unsqueeze(1).to_broadcast([P, NT, 4, DB]), ALU.mult)\
                     .then_inc(b_rp.sem, 1)
                    done(e, b_rp, l)
                    settle(e, e_hold)
                b_pass(en, e, l, 0, True)
                with e.Fori(1, B) as b:
                    b_pass(en, e, l, b, False)
                b_end(en, e, l)
                barrier(e, l * 2 + 2)
                done(e, e_w1, l)
                settle(e, e_hold)
                with e.Fori(0, B) as b:
                    f_pass(en, e, l, b)
                barrier(e, l * 2 + 3)
            if en == "dve":
                for b0 in range(0, 2):
                    lo, hi = b0 * B // 2, (b0 + 1) * B // 2
                    y = xr[:, lo * NT:hi * NT, :].rearrange("p (b t) m -> p b t m", t=NT)
                    e.tensor_tensor(y, y, gb[:, lo:hi, :].unsqueeze(2).to_broadcast([P, B // 2, NT, M]),
                                    ALU.mult).then_inc(o_m.sem, 1)
                done(e, o_m, 0, 1)
                e.tensor_tensor(x1[:, :, :], x1[:, :, :], xr[:, :, :], ALU.add).then_inc(o_m.sem, 1)

        def load_layer_attention(e, l):
            row = lambda a, n: a[bass.ds(l, 1), n].to_broadcast([P, n.stop - n.start])
            lo, hi, full = slice(0, DB // 2), slice(DB // 2, DB), slice(0, DB)
            e.dma_start(wqkvB[:, :, :], Wqkv[bass.ds(l, 1), :, :].rearrange("o m (n c) -> (o m) n c", n=3))\
             .then_inc(e_wq.sem, 16)
            e.dma_start(woB[:, :, :], Wo[bass.ds(l, 1), :, :].rearrange("o (k p) m -> p (o k) m", p=P))\
             .then_inc(e_wq.sem, 16)
            for n, a in enumerate((q_scale, k_scale)):
                e.dma_start(qks[:, 2 * n, full], row(a, full)).then_inc(e_wq.sem, 16)
                e.dma_start(qks[:, 2 * n + 1, lo], row(a, hi)).then_inc(e_wq.sem, 16)
                e.dma_start(qks[:, 2 * n + 1, hi], row(a, lo)).then_inc(e_wq.sem, 16)

        def load_layer_feed_forward(e, l):
            e.dma_start(w1[:, :], W1[bass.ds(l, 1), :, :].rearrange("o m f -> (o m) f")).then_inc(e_w1.sem, 16)
            for n in range(3):
                k = min(P, F - n * P)
                e.dma_start(w2[0:k, n, :], W2[bass.ds(l, 1), n * P:n * P + k, :].rearrange("o f m -> (o f) m"))\
                 .then_inc(e_w1.sem, 16)
            e.dma_start(b1r[:, :], b1[bass.ds(l, 1), :]).then_inc(e_w1.sem, 16)
            e.dma_start(b2r[:, :], b2[bass.ds(l, 1), :]).then_inc(e_w1.sem, 16)
            e.dma_start(lng[:, :], ln_g[bass.ds(l, 1), :].rearrange("o m -> m o")).then_inc(e_w1.sem, 16)
            e.dma_start(lnb[:, :], ln_b[bass.ds(l, 1), :].rearrange("o m -> m o")).then_inc(e_w1.sem, 16)

        @block.sync
        def _(e):
            for x_ in events:
                if x_.credit:
                    e.sem_inc(x_.sem, x_.credit)
            e.dma_start(x0[:, :, :], x.rearrange("b (t p) m -> p (b t) m", p=P)).then_inc(e_const.sem, 16)
            for n, w in enumerate((wq, wk, wv)):
                e.dma_start(wqkvA[:, n, :], w.rearrange("m h d -> m (h d)")).then_inc(e_const.sem, 16)
            e.dma_start(woA[:, :, :], wo.rearrange("h d m -> d h m")).then_inc(e_const.sem, 16)
            for dst, src in ((ropeA[:, :, :, :], ropeA_in), (ropeB[:, :, :, :], ropeB_in), (ident[:, :], ident_in),
                             (mask_f[:, :, :], masks_in), (cr[:, :], c), (wm[:, :], wmod)):
                e.dma_start(dst, src).then_inc(e_const.sem, 16)
            with e.Fori(0, DEPTH) as l:
                e.wait_ge(e_bar.sem, l * 8 + 4)
                settle(e, e_hold)
                load_layer_attention(e, l)
                e.wait_ge(e_bar.sem, l * 8 + 8)
                settle(e, e_hold)
                load_layer_feed_forward(e, l)
                with e.Fori(0, B) as b:
                    for g in range(GROUPS):
                        move_values(e, l * B + b, g)
            done(e, o_m, 0, 2)
            e.dma_start(out.rearrange("b (t p) m -> p (b t) m", p=P), x1[:, :, :]).then_inc(o_out.sem, 16)
            done(e, o_out, 0)

        @block.gpsimd
        def _(e):
            run("pool", e)

        @block.vector
        def _(e):
            e.memset(ones[:, :], 1.0)
            e.memset(xsT[64:P, 0:1], 0.0)
            e.memset(pt[:, :, :, :, :, :], 0.0)
            for g in range(GROUPS):
                e.memset(qd[g][:, :, :, :], 0.0)
                e.memset(kT[g][:, :, 0:WIN], 0.0)
                e.memset(vs[g][0:WIN, 0, :], 0.0)
            done(e, e_const, 0)
            e.tensor_copy(ident16[:, :], ident[:, :])
            e.tensor_copy(maskA[:, :], mask_f[:, 0, 0:3 * P])
            e.tensor_copy(maskB[:, :], mask_f[:, 1, :]).then_inc(e_set.sem, 1)
            run("dve", e)

        @block.scalar
        def _(e):
            run("act", e)

        @block.tensor
        def _(e):
            run("pe", e)


def tables():
    f = np.float32
    pos = np.arange(T, dtype=f)
    half = DA // 2
    freq = np.power(f(10000.0), (-np.arange(half) / f(half)).astype(f)).astype(f)
    rad = (pos[:, None] * freq[None, :]).astype(f)
    c, s = np.cos(rad).astype(f), np.sin(rad).astype(f)
    ropeA = np.stack([np.concatenate([c, c], -1), np.concatenate([-s, s], -1)], 1)
    hb = np.arange(0, DB, 2, dtype=f)
    inv = (f(1.0) / np.power(f(10000.0), hb / f(DB))).astype(f)
    rad = (pos[:, None] * inv[None, :]).astype(f)
    c, s = np.cos(rad).astype(f), np.sin(rad).astype(f)
    base = ((hb + f(0.4 * DB)) / f(1.4 * DB)).astype(f)
    power = ((pos - T // 2) / f(WIN // 2)).astype(f)
    sc = np.power(base[None, :], power[:, None]).astype(f)
    iv = (f(1.0) / sc).astype(f)
    cat = lambda a, b: np.concatenate([a, b], -1)
    ropeB = np.stack([cat(c * sc, c * sc), cat(-s * sc, s * sc), cat(c * iv, c * iv), cat(-s * iv, s * iv)], 1)
    lay = lambda a: np.ascontiguousarray(a.reshape(NT, P, *a.shape[1:]).transpose(1, 0, 2, 3).astype(f))
    q, k = np.arange(P)[:, None], np.arange(P)[None, :]
    diag = np.where(q < k, f(NEG), f(0))
    maskA = np.concatenate([diag, np.zeros((P, P), f), diag, np.zeros((P, P), f)], 1)
    maskB = np.zeros((2, 2, WIN, 2, NW // 2, 2 * WIN), f)
    r, kk = np.arange(WIN)[:, None], np.arange(2 * WIN)[None, :]
    band = np.where((kk < r) | (kk > r + WIN), f(NEG), f(0))
    maskB += band[None, None, :, None, None, :]
    maskB[0, :, :, :, 0, :WIN] = NEG
    masks = np.ascontiguousarray(np.stack([maskA, maskB.reshape(P, CH)], 1).astype(f))
    return np.eye(P, dtype=f), masks, lay(ropeA), lay(ropeB)


_INS = ["L0_attn_x", "L0_attn_wq", "L0_attn_wk", "L0_attn_wv", "L0_attn_wo", "L0_ffn_Wqkv", "L0_ffn_q_scale",
        "L0_ffn_k_scale", "L0_ffn_Wo", "L0_ffn_ln_g", "L0_ffn_ln_b", "L0_ffn_W1", "L0_ffn_b1", "L0_ffn_W2",
        "L0_ffn_b2", "L0_c", "L0_wmod"]


def kernel(**inputs):
    import concourse.bacc as bacc
    from concourse.bass_utils import run_bass_kernel_spmd

    nc = bacc.Bacc("TRN2", target_bir_lowering=False, num_devices=1)
    arrays = {name: np.ascontiguousarray(inputs[name]) for name in _INS}
    for name, table in zip(("ident", "masks", "rope_a", "rope_b"), tables()):
        arrays[name] = table
    args = []
    for name, a in arrays.items():
        args.append(nc.dram_tensor(f"in_{name}", a.shape, mybir.dt.from_np(a.dtype), kind="ExternalInput").ap())
    args.append(nc.dram_tensor("out_0", (B, T, M), F32, kind="ExternalOutput").ap())
    build(nc, *args)
    r = run_bass_kernel_spmd(nc, [{f"in_{n}": a for n, a in arrays.items()}], core_ids=[0])
    return r.results[0]["out_0"]
```

```python
from contextlib import ExitStack

import numpy as np

import concourse.bass as bass
from concourse import mybir

F32 = mybir.dt.float32
BF16 = mybir.dt.bfloat16
ACT = mybir.ActivationFunctionType
ALU = mybir.AluOpType
AX = mybir.AxisListType

P = 128
B, T, M = 8, 256, 128
NT = T // P
CH = 512
INNER = 1024
GROUPS = INNER // CH
DEPTH, HB, DB, WIN = 6, 16, 64, 32
NW = T // WIN
HA, DA = 8, 128
F = int(M * 4 * 2 / 3)
FCH = [min(P, F - n) for n in range(0, F, P)]
half = M // 2
FT = CH // P
FP = B * NT // FT
NEG = -1.0e30
QK = GROUPS * NT * 2
NCH = GROUPS * NT * 3
UNITS = 4
PAIRS = HB // 2
EPS = 1e-5
NEWTON = 3
RSQRT = 3 + 3 * NEWTON
I32 = mybir.dt.int32
FNORM = 4 + 3 * NEWTON
NORM = 4 + 3 * NEWTON


class Ev:

    def __init__(self, sem, per, credit=0, step=1):
        self.sem, self.per, self.credit, self.step = sem, per, credit, step

    def value(self, it, k):
        return it * (self.per * self.step) + (self.credit + (k + 1) * self.step)


def done(eng, ev, it, k=0):
    v = ev.value(it, k)
    if isinstance(v, int) and v <= ev.credit:
        return
    eng.wait_ge(ev.sem, v)


def settle(eng, ev):
    eng.sem_inc(ev.sem, 1)


def free(eng, ev, it, k, ring):
    done(eng, ev, it, k - ring)


def build(nc, x, wq, wk, wv, wo, Wqkv, q_scale, k_scale, Wo, ln_g, ln_b, W1, b1, W2, b2, c, wmod,
          eye_in, masks_in, ropeA_in, ropeB_in, out):
    with ExitStack() as ctx:
        def sb(name, shape, dt=F32):
            return ctx.enter_context(nc.sbuf_tensor(name, shape, dt))

        def ev(name, per, credit=0, step=1):
            e = Ev(ctx.enter_context(nc.semaphore(name)), per, credit, step)
            events.append(e)
            return e

        events = []
        eye = sb("eye", [P, 3, P])
        ident, down, wrap = (eye[:, n, :] for n in range(3))
        ident16 = sb("ident16", [P, P], BF16)
        mask_f = sb("mask_f", [P, 2, CH])
        maskA = sb("maskA", [P, 3 * P], BF16)
        maskB = sb("maskB", [P, CH], BF16)
        ropeA = sb("ropeA", [P, NT, 2, DA])
        ropeB = sb("ropeB", [P, NT, 4, DB])
        rope = sb("rope", [P, NT, 4, DB])
        qks = sb("qks", [P, 4, DB])
        wqkvA = sb("wqkvA", [P, 3, INNER])
        woA = sb("woA", [P, HA, M])
        wqkvB = sb("wqkvB", [P, 3, INNER])
        woB = sb("woB", [P, PAIRS, M])
        w1 = sb("w1", [P, 2 * F])
        w2 = sb("w2", [P, 3, M])
        b1c = sb("b1c", [P, 2, len(FCH)])
        b2b = sb("b2b", [P, 1, M])
        lng = sb("lng", [P, 1])
        lnb = sb("lnb", [P, 1])
        x0 = sb("x0", [P, B * NT, M])
        x1 = sb("x1", [P, B * NT, M])
        xr = sb("xr", [P, B * NT, M])
        gb = sb("gb", [P, B, M])
        wm = sb("wm", [P, 6 * M])
        cr = sb("cr", [B, M])
        cT = sb("cT", [P, 4, B])
        cb = sb("cb", [P, P])
        mod = sb("mod", [P, 6, M])
        gate = sb("gate", [P, 2, M])
        ga = sb("ga", [P, 2, M])
        stat = sb("stat", [P, NT, 6])
        mv = sb("mv", [P, NT, 2])
        rstd = sb("rstd", [P, NT])
        var = sb("var", [P, NT])
        nt = sb("nt", [P, 2, 32])
        ln = sb("ln", [P, NT, M])
        hm = sb("hm", [P, NT, M])
        xcur = sb("xcur", [P, NT, M])
        hT = sb("hT", [P, T])
        xsT = sb("xsT", [P, T])
        raw = sb("raw", [P, 2, CH])
        sq = sb("sq", [P, 2, CH])
        ra = sb("ra", [P, 4, CH])
        rb = sb("rb", [P, 2, CH])
        qn = sb("qn", [P, 4, CH])
        ss = sb("ss", [P, 4, 8])
        sx = sb("sx", [P, 32])
        rs = sb("rs", [P, 4, 8])
        v = [sb(f"v{g}", [P, NT, CH]) for g in range(GROUPS)]
        vs = [sb(f"vs{g}", [P, NT, CH]) for g in range(GROUPS)]
        qT = [sb(f"qT{g}", [P, 4, T]) for g in range(GROUPS)]
        qd = [sb(f"qd{g}", [P, 4, NW, 2 * WIN]) for g in range(GROUPS)]
        kT = [sb(f"kT{g}", [P, 4, WIN + T]) for g in range(GROUPS)]
        dif = sb("dif", [P, 2, CH])
        pr = sb("pr", [P, 2, CH])
        mx = sb("mx", [P, 2, 8])
        sm = sb("sm", [P, 2, 8])
        rl = sb("rl", [P, 2, 8])
        pt = sb("pt", [P, 2, 4, 2, 2, 2 * WIN])
        ptA = sb("ptA", [P, 2, 3 * P])
        oT = sb("oT", [P, PAIRS, T])
        warm = sb("warm", [1, 2])
        fst = sb("fst", [P, FT, 6])
        fmv = sb("fmv", [P, FT, 2])
        frs = sb("frs", [P, FT])
        fnt = sb("fnt", [P, 3, FT])
        fln = qn[:, 0, :].rearrange("p (t m) -> p t m", t=FT)
        xnT = qn[:, 1, :]
        gel = rb
        fx = raw[:, 0, :].rearrange("p (t m) -> p t m", t=FT)
        gT = ra
        yo = sb("yo", [P, NT, M])

        def bank(name):
            return ctx.enter_context(nc.psum_tensor(name, [P, CH], F32))

        pQ = [bank("pQ0"), bank("pQ1")]
        pT = bank("pT")
        pS = [bank("pS0"), bank("pS1")]
        pP = bank("pP")
        pO = bank("pO")
        pM = bank("pM")
        pV = [pO, pM]

        e_const = ev("e_const", 1, step=16 * 11)
        e_set = ev("e_set", 1)
        e_hold = ev("e_hold", 1)
        e_bar = ev("e_bar", 1)
        a_cT = ev("a_cT", 1)
        a_e = ev("a_e", 1)
        a_si = ev("a_si", 3)
        a_cb = ev("a_cb", 1)
        a_mo = ev("a_mo", 1)
        a_mc = ev("a_mc", 1)
        a_g = ev("a_g", 5)
        a_st = ev("a_st", 4)
        a_h = ev("a_h", 3)
        a_hT = ev("a_hT", 1)
        a_hc = ev("a_hc", 1)
        a_pj = ev("a_pj", NCH, NCH)
        a_ev = ev("a_ev", NCH, 2)
        a_ab = ev("a_ab", QK, 2)
        a_qn = ev("a_qn", QK, 2)
        a_tr = ev("a_tr", QK, 4)
        a_tc = ev("a_tc", QK, 1)
        a_S = ev("a_S", HA, HA)
        a_mx = ev("a_mx", HA)
        a_nm = ev("a_nm", HA)
        a_ex = ev("a_ex", HA, 2)
        a_rl = ev("a_rl", HA)
        a_pn = ev("a_pn", HA)
        a_pt = ev("a_pt", HA, 2)
        a_pc = ev("a_pc", HA, 1)
        a_pv = ev("a_pv", HA, HA)
        a_oc = ev("a_oc", HA, 1)
        a_wo = ev("a_wo", 1, 1)
        a_y = ev("a_y", 2)
        a_s2 = ev("a_s2", 4)
        a_str = ev("a_str", RSQRT)
        a_s2r = ev("a_s2r", RSQRT)
        a_x = ev("a_x", 2)
        e_wq = ev("e_wq", 1, step=16 * 8)
        e_w1 = ev("e_w1", 1, step=16 * 13)
        b_rp = ev("b_rp", 1)
        b_xc = ev("b_xc", 1)
        b_xt = ev("b_xt", 1, 1)
        b_xs = ev("b_xs", 1)
        b_pj = ev("b_pj", NCH, NCH)
        b_ev = ev("b_ev", NCH, 2)
        b_ss = ev("b_ss", QK)
        b_rs = ev("b_rs", GROUPS * NORM)
        b_ab = ev("b_ab", QK, 2)
        b_ad = ev("b_ad", QK, 2)
        b_qn = ev("b_qn", QK, 4)
        b_tr = ev("b_tr", QK, 4)
        b_tc = ev("b_tc", QK, 1)
        b_vs = [ev(f"b_vs{g}", 1, step=16 * 2) for g in range(GROUPS)]
        b_S = ev("b_S", UNITS, UNITS)
        b_mx = ev("b_mx", UNITS)
        b_sub = ev("b_sub", UNITS, 2)
        b_ex = ev("b_ex", UNITS, 2)
        b_sm = ev("b_sm", UNITS)
        b_rl = ev("b_rl", UNITS)
        b_pn = ev("b_pn", UNITS)
        b_pt = ev("b_pt", UNITS, 2)
        b_pc = ev("b_pc", UNITS, 1)
        b_pv = ev("b_pv", PAIRS, PAIRS)
        b_oc = ev("b_oc", PAIRS, 2)
        b_wo = ev("b_wo", 1, 1)
        b_wx = ev("b_wx", 1, 2)
        f_sh = ev("f_sh", 1)
        f_xa = ev("f_xa", 1)
        f_xs = ev("f_xs", 1, 1)
        f_st = ev("f_st", 2)
        f_rs = ev("f_rs", FNORM, 0)
        f_ln = ev("f_ln", 1, 1)
        f_xb = ev("f_xb", 1)
        f_lt = ev("f_lt", 1, 1)
        f_xn = ev("f_xn", 1, 1)
        f_h = ev("f_h", 3, 3)
        f_ge = ev("f_ge", 3)
        f_G = ev("f_G", 3, 3)
        f_y = ev("f_y", 3, 3)
        f_x = ev("f_x", 1, 1)
        o_m = ev("o_m", 3)
        o_out = ev("o_out", 1, step=16)

        block = ctx.enter_context(nc.Block())

        def barrier(eng, n):
            eng.drain().then_inc(e_bar.sem, 1)
            eng.wait_ge(e_bar.sem, (n + 1) * 4)
            settle(eng, e_hold)

        def rsqrt(e, evt, it, n, y, x_, h, t):
            k = [n * RSQRT]

            def then(i):
                i.then_inc(evt.sem, 1)
                done(e, evt, it, k[0])
                k[0] += 1

            then(e.tensor_scalar(t.bitcast(I32), x_.bitcast(I32), 1, None, ALU.arith_shift_right))
            then(e.tensor_scalar(y.bitcast(I32), t.bitcast(I32), -1.0, float(0x5F3759DF), ALU.mult, ALU.add))
            then(e.tensor_scalar(h, x_, -0.5, None, ALU.mult))
            for _ in range(NEWTON):
                then(e.tensor_tensor(t, y, y, ALU.mult))
                then(e.tensor_tensor(t, t, h, ALU.mult))
                then(e.scalar_tensor_tensor(y, t, 1.5, y, ALU.add, ALU.mult))

        def chunk(c):
            return c // 6, (c % 6) // 3, c % 3

        def a_front(en, e, b):
            if en == "dve":
                done(e, a_si, 0, 2)
                if not (isinstance(b, int) and b == 0):
                    done(e, a_mo, b - 1)
                e.tensor_copy(cb[:, :], cT[:, 3, bass.ds(b, 1)].to_broadcast([P, P])).then_inc(a_cb.sem, 1)
                xin = x0[:, bass.ds(b * NT, NT), :]
                settle(e, e_hold)
                for t in range(NT):
                    i = e.bn_stats(stat[:, t, :], xin[:, t, :])
                i.then_inc(a_st.sem, 1)
                done(e, a_st, b, 0)
                settle(e, e_hold)
                for t in range(NT):
                    i = e.bn_aggr(mv[:, t, :], stat[:, t, :])
                i.then_inc(a_st.sem, 1)
                done(e, a_st, b, 1)
                e.tensor_scalar(var[:, :], mv[:, :, 1], EPS, None, ALU.add).then_inc(a_st.sem, 1)
                done(e, a_st, b, 2)
                rsqrt(e, a_str, b, 0, rstd[:, :], var[:, :], nt[:, 0, 0:NT], nt[:, 1, 0:NT])
                for t in range(NT):
                    i = e.tensor_scalar(ln[:, t, :], xin[:, t, :], mv[:, t, 0:1], rstd[:, t:t + 1],
                                        ALU.subtract, ALU.mult)
                i.then_inc(a_st.sem, 1)
                done(e, a_mc, b)
                g3 = mod[:, 2::3, :]
                e.tensor_scalar(gate[:, :, :], g3, 0.0, 2.0, ALU.is_ge, ALU.mult).then_inc(a_g.sem, 1)
                done(e, a_g, b, 0)
                e.tensor_scalar(gate[:, :, :], gate[:, :, :], -1.0, None, ALU.add).then_inc(a_g.sem, 1)
                e.scalar_tensor_tensor(ga[:, :, :], g3, -1.0, g3, ALU.mult, ALU.max).then_inc(a_g.sem, 1)
                e.tensor_scalar(mod[:, 1::3, :], mod[:, 1::3, :], 1.0, None, ALU.add).then_inc(a_g.sem, 1)
                done(e, a_g, b, 3)
                e.scalar_tensor_tensor(gate[:, :, :], ga[:, :, :], 0.25, gate[:, :, :], ALU.max, ALU.mult)\
                 .then_inc(a_g.sem, 1)
                done(e, a_st, b, 3)
                e.tensor_tensor(ln[:, :, :], ln[:, :, :], mod[:, 1:2, :].to_broadcast([P, NT, M]),
                                ALU.mult).then_inc(a_h.sem, 1)
                done(e, a_h, b, 0)
                e.tensor_tensor(hm[:, :, :], ln[:, :, :], mod[:, 0:1, :].to_broadcast([P, NT, M]),
                                ALU.add).then_inc(a_h.sem, 1)
                done(e, a_g, b, 4)
                e.tensor_copy(gb[:, bass.ds(b, 1), :], gate[:, 1:2, :]).then_inc(a_h.sem, 1)
            if en == "pe":
                done(e, a_cb, b)
                free(e, a_ev, b, 1, 2)
                for n in range(2):
                    i = e.matmul(pQ[n][:, 0:3 * M], cb[:, :], wm[:, n * 3 * M:(n + 1) * 3 * M],
                                 start=True, stop=True)
                i.then_inc(a_mo.sem, 1)
                done(e, a_h, b, 1)
                for t in range(NT):
                    i = e.transpose(pM[:, t * M:(t + 1) * M], hm[:, t, :], ident)
                i.then_inc(a_hT.sem, 1)
            if en == "act":
                done(e, a_mo, b)
                if not (isinstance(b, int) and b == 0):
                    done(e, a_x, b - 1, 1)
                for n in range(2):
                    i = e.copy(mod[:, 3 * n:3 * n + 3, :], pQ[n][:, 0:3 * M])
                i.then_inc(a_mc.sem, 1)
                done(e, a_hT, b)
                free(e, a_pj, b, 11, NCH)
                e.copy(hT[:, :], pM[:, 0:T]).then_inc(a_hc.sem, 1)

        def a_chunk(en, e, b, c_):
            g, t, kind = chunk(c_)
            j = g * 4 + t * 2 + kind
            if en == "pe":
                if c_ == 0:
                    done(e, a_hc, b)
                    done(e, a_mc, b)
                free(e, a_ev, b, c_, 2)
                e.matmul(pQ[c_ % 2][:, :], hT[:, t * P:(t + 1) * P], wqkvA[:, kind, g * CH:(g + 1) * CH],
                         start=True, stop=True).then_inc(a_pj.sem, 1)
            if en == "act":
                done(e, a_pj, b, c_)
                if kind == 2:
                    free(e, a_pv, b, 4 * g + 3, HA)
                    e.copy(v[g][:, t, :], pQ[c_ % 2][:, :]).then_inc(a_ev.sem, 1)
                else:
                    free(e, a_ab, b, j, 2)
                    e.copy(raw[:, j % 2, :], pQ[c_ % 2][:, :]).then_inc(a_ev.sem, 1)
            if en == "dve" and kind < 2:
                done(e, a_ev, b, c_)
                r = raw[:, j % 2, :].rearrange("p (h s d) -> p h s d", s=2, d=DA // 2)
                shape = [P, 4, 2, DA // 2]
                cos, sin = (ropeA[:, t:t + 1, n, :].rearrange("p o (s d) -> p o s d", s=2).to_broadcast(shape)
                            for n in range(2))
                free(e, a_qn, b, j, 2)
                oa, ob = (y[:, j % 2, :].rearrange("p (h s d) -> p h s d", s=2, d=DA // 2) for y in (ra, rb))
                e.tensor_tensor(oa, r, cos, ALU.mult)
                e.tensor_tensor(ob, r[:, :, ::-1, :], sin, ALU.mult).then_inc(a_ab.sem, 1)
            if en == "pool" and kind < 2:
                done(e, a_ab, b, j)
                free(e, a_tr, b, j, 4)
                e.tensor_tensor(qn[:, j % 4, :], ra[:, j % 2, :], rb[:, j % 2, :], ALU.add).then_inc(a_qn.sem, 1)

        def a_turn(en, e, b, j):
            g, t, isk = j // 4, (j % 4) // 2, j % 2
            if en == "pe":
                done(e, a_qn, b, j)
                free(e, a_tc, b, j, 1)
                for h in range(4):
                    i = e.transpose(pT[:, h * P:(h + 1) * P], qn[:, j % 4, h * P:(h + 1) * P], ident)
                i.then_inc(a_tr.sem, 1)
            if en == "act":
                done(e, a_tr, b, j)
                free(e, a_S, b, 4 * g + 3, HA)
                dst = kT[g][:, :, WIN + t * P:WIN + (t + 1) * P] if isk else qT[g][:, :, t * P:(t + 1) * P]
                e.copy(dst, pT[:, :].rearrange("p (h q) -> p h q", h=4)).then_inc(a_tc.sem, 1)

        def a_scores(en, e, b, h):
            g, s = h // 4, h % 2
            rows = ((0, P), (P, 3 * P))
            if en == "pe":
                done(e, a_tc, b, 4 * g + 3)
                free(e, a_ex, b, h, 2)
                e.matmul(pS[s][:, 0:3 * P], ident16[:, :], maskA[:, :], start=True, stop=False,
                         skip_group_check=True)
                for t, (lo, hi) in enumerate(rows):
                    i = e.matmul(pS[s][:, lo:hi], qT[g][:, h % 4, t * P:(t + 1) * P],
                                 kT[g][:, h % 4, WIN:WIN + (t + 1) * P], start=False, stop=True,
                                 skip_group_check=True)
                i.then_inc(a_S.sem, 1)
            if en == "dve":
                done(e, a_S, b, h)
                for t, (lo, hi) in enumerate(rows):
                    i = e.tensor_reduce(mx[:, s, t:t + 1], pS[s][:, lo:hi], AX.X, ALU.max)
                i.then_inc(a_mx.sem, 1)
                done(e, a_mx, b, h)
                e.tensor_scalar(mx[:, s, 2:4], mx[:, s, 0:2], -1.0 / DA, None, ALU.mult).then_inc(a_nm.sem, 1)
            if en == "act":
                done(e, a_nm, b, h)
                free(e, a_pt, b, h, 2)
                for t, (lo, hi) in enumerate(rows):
                    i = e.activation(pr[:, s, lo:hi], pS[s][:, lo:hi], ACT.Exp, bias=mx[:, s, 2 + t:3 + t],
                                     scale=1.0 / DA, accum_out=sm[:, s, t:t + 1])
                i.then_inc(a_ex.sem, 1)

        def a_norm(en, e, b, h):
            s = h % 2
            if en == "dve":
                done(e, a_ex, b, h)
                e.reciprocal(rl[:, s, 0:2], sm[:, s, 0:2]).then_inc(a_rl.sem, 1)
                done(e, a_rl, b, h)
                for t, (lo, hi) in enumerate(((0, P), (P, 3 * P))):
                    i = e.tensor_scalar(pr[:, s, lo:hi], pr[:, s, lo:hi], rl[:, s, t:t + 1], None, ALU.mult)
                i.then_inc(a_pn.sem, 1)

        def a_values(en, e, b, h):
            g, s = h // 4, h % 2
            if en == "pe":
                done(e, a_pn, b, h)
                free(e, a_pc, b, h, 1)
                for n in range(3):
                    i = e.transpose(pP[:, n * P:(n + 1) * P], pr[:, s, n * P:(n + 1) * P], ident)
                i.then_inc(a_pt.sem, 1)
                done(e, a_pc, b, h)
                done(e, a_ev, b, g * 6 + 5)
                free(e, a_oc, b, h, 1)
                for n, (q, k) in enumerate(((0, 0), (1, 0), (1, 1))):
                    i = e.matmul(pO[:, q * P:(q + 1) * P], v[g][:, k, (h % 4) * P:(h % 4 + 1) * P],
                                 ptA[:, s, n * P:(n + 1) * P], start=(k == 0), stop=(k == q))
                i.then_inc(a_pv.sem, 1)
            if en == "act":
                done(e, a_pt, b, h)
                free(e, a_pv, b, h, 2)
                e.copy(ptA[:, s, :], pP[:, 0:3 * P]).then_inc(a_pc.sem, 1)
                done(e, a_pv, b, h)
                if h == 0:
                    free(e, a_wo, b, 0, 1)
                e.copy(oT[:, h, :], pO[:, 0:T]).then_inc(a_oc.sem, 1)

        def a_out(en, e, b):
            if en == "pe":
                done(e, a_oc, b, HA - 1)
                done(e, a_hc, b)
                for t in range(NT):
                    for h in range(HA):
                        i = e.matmul(pM[:, t * M:(t + 1) * M], oT[:, h, t * P:(t + 1) * P], woA[:, h, :],
                                     start=(h == 0), stop=(h == HA - 1))
                i.then_inc(a_wo.sem, 1)
            if en == "dve":
                done(e, a_wo, b)
                xi, xo = x0[:, bass.ds(b * NT, NT), :], x1[:, bass.ds(b * NT, NT), :]
                e.tensor_tensor(yo[:, :, :], pM[:, 0:T].rearrange("p (t m) -> p t m", t=NT),
                                gate[:, 0:1, :].to_broadcast([P, NT, M]), ALU.mult).then_inc(a_y.sem, 1)
                done(e, a_y, b, 0)
                e.tensor_tensor(xo, xi, yo[:, :, :], ALU.add).then_inc(a_y.sem, 1)
                done(e, a_y, b, 1)
                settle(e, e_hold)
                for t in range(NT):
                    i = e.bn_stats(stat[:, t, :], xo[:, t, :])
                i.then_inc(a_s2.sem, 1)
                done(e, a_s2, b, 0)
                settle(e, e_hold)
                for t in range(NT):
                    i = e.bn_aggr(mv[:, t, :], stat[:, t, :])
                i.then_inc(a_s2.sem, 1)
                done(e, a_s2, b, 1)
                e.tensor_scalar(var[:, :], mv[:, :, 1], EPS, None, ALU.add).then_inc(a_s2.sem, 1)
                done(e, a_s2, b, 2)
                rsqrt(e, a_s2r, b, 0, rstd[:, :], var[:, :], nt[:, 0, 0:NT], nt[:, 1, 0:NT])
                for t in range(NT):
                    i = e.tensor_scalar(ln[:, t, :], xo[:, t, :], mv[:, t, 0:1], rstd[:, t:t + 1],
                                        ALU.subtract, ALU.mult)
                i.then_inc(a_s2.sem, 1)
                done(e, a_s2, b, 3)
                e.tensor_tensor(ln[:, :, :], ln[:, :, :], mod[:, 4:5, :].to_broadcast([P, NT, M]),
                                ALU.mult).then_inc(a_x.sem, 1)
                done(e, a_x, b, 0)
                e.tensor_tensor(xr[:, bass.ds(b * NT, NT), :], ln[:, :, :],
                                mod[:, 3:4, :].to_broadcast([P, NT, M]), ALU.add).then_inc(a_x.sem, 1)

        def a_pass(en, e, b):
            a_front(en, e, b)
            for c_ in range(6):
                a_chunk(en, e, b, c_)
            for j in range(4):
                a_turn(en, e, b, j)
            for c_ in range(6, 12):
                a_chunk(en, e, b, c_)
                if c_ < 10:
                    a_scores(en, e, b, c_ - 6)
                if 7 <= c_ < 11:
                    a_norm(en, e, b, c_ - 7)
                if c_ >= 8:
                    a_values(en, e, b, c_ - 8)
            for j in range(4, 8):
                a_turn(en, e, b, j)
            for h in range(4, 10):
                if h < 8:
                    a_scores(en, e, b, h)
                if 5 <= h < 9:
                    a_norm(en, e, b, h - 1)
                if h >= 6:
                    a_values(en, e, b, h - 2)
            a_out(en, e, b)


        def xt_copy(e, it, b):
            free(e, b_xt, it, 0, 1)
            settle(e, e_hold)
            e.tensor_copy(xcur[:, :, :], xr[:, bass.ds(b * NT, NT), :]).then_inc(b_xc.sem, 1)

        def xt_turn(e, it):
            done(e, b_xc, it)
            free(e, b_wx, it, 0, 2)
            for t in range(NT):
                i = e.transpose(pM[:, t * M:(t + 1) * M], xcur[:, t, :], ident)
            i.then_inc(b_xt.sem, 1)

        def xt_shift(e, it):
            done(e, b_xt, it)
            free(e, b_pj, it, NCH - 1, NCH)
            e.copy(xsT[0:64, :], pM[0:64, 0:T])
            e.copy(xsT[64:P, 1:T], pM[64:P, 0:T - 1]).then_inc(b_xs.sem, 1)

        def proj(e, it, c_):
            g, t, kind = chunk(c_)
            if c_ == 0:
                done(e, b_xs, it)
            free(e, b_ev, it, c_, 2)
            e.matmul(pQ[c_ % 2][:, :], xsT[:, t * P:(t + 1) * P], wqkvB[:, kind, g * CH:(g + 1) * CH],
                     start=True, stop=True).then_inc(b_pj.sem, 1)

        def evacuate(e, it, c_):
            g, t, kind = chunk(c_)
            j = g * 4 + t * 2 + kind
            done(e, b_pj, it, c_)
            if kind == 2:
                free(e, b_pv, it, 4 * g + 3, PAIRS)
                e.copy(v[g][:, t, :], pQ[c_ % 2][:, :]).then_inc(b_ev.sem, 1)
            else:
                free(e, b_ab, it, j, 2)
                e.copy(raw[:, j % 2, :], pQ[c_ % 2][:, :])
                e.activation(sq[:, j % 2, :], pQ[c_ % 2][:, :], ACT.Square).then_inc(b_ev.sem, 1)

        def rotate(e, it, j):
            g, t, kind = j // 4, (j % 4) // 2, j % 2
            done(e, b_ev, it, g * 6 + t * 3 + kind)
            e.tensor_reduce(ss[:, j % 4, :], sq[:, j % 2, :].rearrange("p (h d) -> p h d", d=DB),
                            AX.X, ALU.add).then_inc(b_ss.sem, 1)
            free(e, b_ad, it, j, 2)
            free(e, b_qn, it, j, 4)
            r = raw[:, j % 2, :].rearrange("p (h s d) -> p h s d", s=2, d=DB // 2)
            shape = [P, 8, 2, DB // 2]
            cos, sin = (rope[:, t:t + 1, 2 * kind + n, :].rearrange("p o (s d) -> p o s d", s=2)
                        .to_broadcast(shape) for n in range(2))
            oa, ob = (y.rearrange("p (h s d) -> p h s d", s=2, d=DB // 2)
                      for y in (ra[:, j % 4, :], rb[:, j % 2, :]))
            e.tensor_tensor(oa, r, cos, ALU.mult)
            e.tensor_tensor(ob, r[:, :, ::-1, :], sin, ALU.mult).then_inc(b_ab.sem, 1)

        def rotate_add(e, it, j):
            done(e, b_ab, it, j)
            e.tensor_tensor(ra[:, j % 4, :], ra[:, j % 4, :], rb[:, j % 2, :], ALU.add).then_inc(b_ad.sem, 1)

        flat = lambda y: y.rearrange("p n h -> p (n h)")
        x_, y_ = flat(ss[:, :, :]), flat(rs[:, :, :])

        def norm_chain(e, it, g):
            k = [g * NORM]

            def then(i):
                i.then_inc(b_rs.sem, 1)
                k[0] += 1

            def before():
                done(e, b_rs, it, k[0] - 1)

            t, h = nt[:, 0, :], nt[:, 1, :]
            done(e, b_ss, it, 4 * g + 3)
            then(e.tensor_scalar(sx[:, :], x_, 1e-24, None, ALU.max))
            yield
            before()
            then(e.tensor_scalar(t.bitcast(I32), sx[:, :].bitcast(I32), 1, None, ALU.arith_shift_right))
            yield
            before()
            then(e.tensor_scalar(y_.bitcast(I32), t.bitcast(I32), -1.0, float(0x5F3759DF), ALU.mult, ALU.add))
            then(e.tensor_scalar(h, sx[:, :], -0.5, None, ALU.mult))
            yield
            for _ in range(NEWTON):
                before()
                then(e.tensor_tensor(t, y_, y_, ALU.mult))
                yield
                before()
                then(e.tensor_tensor(t, t, h, ALU.mult))
                yield
                before()
                then(e.scalar_tensor_tensor(y_, t, 1.5, y_, ALU.add, ALU.mult))
                yield

        def normalise(e, it, j):
            done(e, b_ad, it, j)
            done(e, b_rs, it, (j // 4) * NORM + NORM - 1)
            free(e, b_tr, it, j, 4)
            e.tensor_tensor(qn[:, j % 4, :].rearrange("p (h d) -> p h d", d=DB),
                            ra[:, j % 4, :].rearrange("p (h d) -> p h d", d=DB),
                            rs[:, j % 4, :].unsqueeze(2).to_broadcast([P, 8, DB]), ALU.mult)\
             .then_inc(b_qn.sem, 1)

        def turn(e, it, j):
            done(e, b_qn, it, j)
            free(e, b_tc, it, j, 1)
            for p in range(4):
                i = e.transpose(pT[:, p * P:(p + 1) * P], qn[:, j % 4, p * P:(p + 1) * P], ident)
            i.then_inc(b_tr.sem, 1)

        def turn_copy(e, it, j):
            g, t, isk = j // 4, (j % 4) // 2, j % 2
            done(e, b_tr, it, j)
            if j % 4 == 0:
                free(e, b_S, it, 2 * g + 1, UNITS)
            if isk:
                e.copy(kT[g][:, :, WIN + t * P:WIN + (t + 1) * P],
                       pT[:, :].rearrange("p (h q) -> p h q", h=4)).then_inc(b_tc.sem, 1)
            else:
                for s in range(2):
                    i = e.copy(qd[g][64 * s:64 * s + 64, :, 4 * t:4 * t + 4, WIN * s:WIN * s + WIN],
                               pT[64 * s:64 * s + 64, :].rearrange("p (h w q) -> p h w q", h=4, w=4))
                i.then_inc(b_tc.sem, 1)

        def scores(e, it, u):
            g, s = u // 2, u % 2
            done(e, b_tc, it, 4 * g + 3)
            free(e, b_sub, it, u, 2)
            e.matmul(pS[s][:, :], ident16[:, :], maskB[:, :], start=True, stop=False, skip_group_check=True)
            for p2 in range(2):
                for w in range(NW):
                    lo = p2 * 256 + (w // 2) * 64
                    i = e.matmul(pS[s][64 * (w % 2):64 * (w % 2) + 64, lo:lo + 64],
                                 qd[g][:, 2 * (u % 2) + p2, w, :],
                                 kT[g][:, 2 * (u % 2) + p2, WIN * w:WIN * w + 2 * WIN],
                                 start=False, stop=True, skip_group_check=True)
            i.then_inc(b_S.sem, 1)

        def less_max(e, it, u):
            s = u % 2
            done(e, b_S, it, u)
            sc = pS[s][:, :].rearrange("p (n k) -> p n k", k=64)
            e.tensor_reduce(mx[:, s, :], sc, AX.X, ALU.max).then_inc(b_mx.sem, 1)
            done(e, b_mx, it, u)
            free(e, b_ex, it, u, 2)
            e.tensor_tensor(dif[:, s, :].rearrange("p (n k) -> p n k", k=64), sc,
                            mx[:, s, :].unsqueeze(2).to_broadcast([P, 8, 64]), ALU.subtract)\
             .then_inc(b_sub.sem, 1)

        def exponent(e, it, u):
            s = u % 2
            done(e, b_sub, it, u)
            free(e, b_pt, it, u, 2)
            e.activation(pr[:, s, :], dif[:, s, :], ACT.Exp, scale=8.0).then_inc(b_ex.sem, 1)

        def row_sums(e, it, u):
            s = u % 2
            done(e, b_ex, it, u)
            e.tensor_reduce(sm[:, s, :], pr[:, s, :].rearrange("p (n k) -> p n k", k=64),
                            AX.X, ALU.add).then_inc(b_sm.sem, 1)
            done(e, b_sm, it, u)
            e.reciprocal(rl[:, s, :], sm[:, s, :]).then_inc(b_rl.sem, 1)

        def soft_norm(e, it, u):
            s = u % 2
            done(e, b_rl, it, u)
            y = pr[:, s, :].rearrange("p (n k) -> p n k", k=64)
            e.tensor_tensor(y, y, rl[:, s, :].unsqueeze(2).to_broadcast([P, 8, 64]), ALU.mult)\
             .then_inc(b_pn.sem, 1)

        def turn_p(e, it, u):
            done(e, b_pn, it, u)
            free(e, b_pc, it, u, 1)
            for n in range(4):
                i = e.transpose(pP[:, n * P:(n + 1) * P], pr[:, u % 2, n * P:(n + 1) * P], ident)
            i.then_inc(b_pt.sem, 1)

        def copy_p(e, it, u):
            done(e, b_pt, it, u)
            free(e, b_pv, it, 2 * u + 1, 4)
            dst = pt[:, u % 2, :, :, :, :].rearrange("p n a b k -> p (n a) b k")
            src = pP[:, :].rearrange("p (n k) -> p n k", k=64)
            for h in range(2):
                i = e.copy(dst[64 * h:64 * h + 64, :, h, :], src[64 * h:64 * h + 64, :, :])
            i.then_inc(b_pc.sem, 1)

        def values(e, it, k, first=False, nxt=True):
            u, g, p2, pair = k // 2, k // 4, k % 2, k % 4
            if p2 == 0:
                done(e, b_pc, it, u)
            if pair == 0:
                done(e, b_ev, it, g * 6 + 5)
                done(e, b_vs[g], it)
            free(e, b_oc, it, k, 2)
            if k == 0 and not first:
                done(e, b_wx, it - 1)
            if k == 1 and nxt:
                done(e, b_xs, it + 1)
            o = pV[k % 2][:, :].rearrange("p (t a c q) -> p t a c q", t=NT, a=2, c=2)
            for t in range(NT):
                for par in range(2):
                    i = e.matmul(o[:, t, :, par, :], (v if par else vs)[g][:, t, pair * P:(pair + 1) * P],
                                 pt[:, u % 2, 2 * p2 + t, par, :, :], start=(t == 0 and par == 0), stop=True,
                                 skip_group_check=True)
            i.then_inc(b_pv.sem, 1)

        def copy_o(e, it, k):
            done(e, b_pv, it, k)
            if k == 0:
                free(e, b_wo, it, 0, 1)
            o = pV[k % 2][:, :].rearrange("p (w h q) -> p w h q", h=2, q=WIN)
            for h in range(2):
                i = e.copy(oT[64 * h:64 * h + 64, k, :].rearrange("p (w q) -> p w q", q=WIN),
                           o[64 * h:64 * h + 64, :, h, :])
            i.then_inc(b_oc.sem, 1)

        def out_proj(e, it):
            done(e, b_oc, it, PAIRS - 1)
            for t in range(NT):
                for k in range(PAIRS):
                    i = e.matmul(pO[:, t * M:(t + 1) * M], oT[:, k, t * P:(t + 1) * P], woB[:, k, :],
                                 start=(k == 0), stop=(k == PAIRS - 1))
            i.then_inc(b_wo.sem, 1)

        def out_add(e, it, b):
            done(e, b_wo, it)
            xd = xr[:, bass.ds(b * NT, NT), :]
            e.tensor_tensor(xd, pO[:, 0:T].rearrange("p (t m) -> p t m", t=NT), xd, ALU.add)\
             .then_inc(b_wx.sem, 1)

        def move_values(e, it, g):
            done(e, b_ev, it, g * 6 + 5)
            settle(e, e_hold)
            free(e, b_pv, it, 4 * g + 3, PAIRS)
            settle(e, e_hold)
            e.dma_start(vs[g][WIN:P, :, :], v[g][0:P - WIN, :, :]).then_inc(b_vs[g].sem, 16)
            e.dma_start(vs[g][0:WIN, 1, :], v[g][P - WIN:P, 0, :]).then_inc(b_vs[g].sem, 16)

        def slot(en, e, it, b, g, F_, K_, L_, first=False, nxt=False):
            ib, gb_ = (it, g - 1) if g else (it - 1, GROUPS - 1)
            il, gl = it - 1, g
            c0, j0 = 6 * g, 4 * g
            jb, u0, k0 = 4 * gb_, 2 * gb_, 4 * gb_
            ul, kl = 2 * gl + 1, 4 * gl + 2
            steps = []
            F = lambda f, *a: steps.append((F_, f, a))
            K = lambda f, *a: steps.append((K_, f, a))
            L = lambda f, *a: steps.append((L_, f, a))
            if en == "pe":
                F(proj, it, c0)
                L(turn_p, il, ul)
                K(turn, ib, jb)
                F(proj, it, c0 + 1)
                K(turn, ib, jb + 1)
                L(values, il, kl)
                K(turn, ib, jb + 2)
                L(values, il, kl + 1)
                K(turn, ib, jb + 3)
                F(proj, it, c0 + 2)
                K(scores, ib, u0)
                F(proj, it, c0 + 3)
                K(scores, ib, u0 + 1)
                F(proj, it, c0 + 4)
                if g:
                    L(out_proj, il)
                if nxt:
                    F(xt_turn, it + 1)
                K(turn_p, ib, u0)
                F(proj, it, c0 + 5)
                K(values, ib, k0, first, nxt)
                K(values, ib, k0 + 1, first, nxt)
            if en == "act":
                F(evacuate, it, c0)
                L(copy_p, il, ul)
                K(turn_copy, ib, jb)
                F(evacuate, it, c0 + 1)
                K(turn_copy, ib, jb + 1)
                L(copy_o, il, kl)
                K(turn_copy, ib, jb + 2)
                L(copy_o, il, kl + 1)
                K(turn_copy, ib, jb + 3)
                F(evacuate, it, c0 + 2)
                F(evacuate, it, c0 + 3)
                K(exponent, ib, u0)
                F(evacuate, it, c0 + 4)
                K(exponent, ib, u0 + 1)
                K(copy_p, ib, u0)
                F(evacuate, it, c0 + 5)
                if nxt:
                    F(xt_shift, it + 1)
                K(copy_o, ib, k0)
                K(copy_o, ib, k0 + 1)
            if en == "dve":
                F(rotate, it, j0)
                F(rotate, it, j0 + 1)
                K(less_max, ib, u0)
                F(rotate, it, j0 + 2)
                K(row_sums, ib, u0)
                F(rotate, it, j0 + 3)
                chain = norm_chain(e, it, g)
                link = lambda *a: next(chain, None)
                F(link)
                K(less_max, ib, u0 + 1)
                for _ in range(6):
                    F(link)
                if g:
                    L(out_add, il, b - 1)
                for _ in range(3):
                    F(link)
                K(row_sums, ib, u0 + 1)
                for _ in range(3):
                    F(link)
                for j in range(4):
                    F(normalise, it, j0 + j)
            if en == "pool":
                F(rotate_add, it, j0)
                F(rotate_add, it, j0 + 1)
                F(rotate_add, it, j0 + 2)
                K(soft_norm, ib, u0)
                F(rotate_add, it, j0 + 3)
                K(soft_norm, ib, u0 + 1)
                if nxt:
                    F(xt_copy, it + 1, b + 1)
            for on, f, a in steps:
                if on:
                    f(e, *a)

        def b_pass(en, e, l, b, first=False, last=False):
            it = l * B + b
            slot(en, e, it, b, 0, True, not first, not first)
            slot(en, e, it, b, 1, True, True, not first, first, not last)

        def b_attention(en, e, l):
            if en == "pool":
                xt_copy(e, l * B, 0)
            if en == "pe":
                xt_turn(e, l * B)
            if en == "act":
                xt_shift(e, l * B)
            b_pass(en, e, l, 0, first=True)
            with e.Fori(1, B - 1) as b:
                b_pass(en, e, l, b)
            b_pass(en, e, l, B - 1, last=True)
            slot(en, e, (l + 1) * B, B, 0, False, True, True)
            slot(en, e, (l + 1) * B, B, 1, False, False, True)

        tiles = lambda f: bass.ds(f * FT, FT)

        def l_shift(e, it, f):
            free(e, f_xs, it, 0, 1)
            e.matmul(pM[:, 0:FT * half], down, xr[:, tiles(f), half:M], start=True, stop=False,
                     skip_group_check=True)
            o = pM[:, 0:FT * half].rearrange("p (b t m) -> p b t m", t=NT, m=half)
            e.matmul(o[:, :, 1, :], wrap, xr[:, tiles(f), half:M].rearrange("p (b t) m -> p b t m", t=NT)[:, :, 0, :],
                     start=False, stop=True, skip_group_check=True).then_inc(f_sh.sem, 1)

        def l_first(e, it, f):
            free(e, f_ln, it, 0, 1)
            settle(e, e_hold)
            e.tensor_copy(fx[:, :, 0:half], xr[:, tiles(f), 0:half]).then_inc(f_xa.sem, 1)

        def l_second(e, it):
            done(e, f_sh, it)
            free(e, f_ln, it, 0, 1)
            e.tensor_copy(fx[:, :, half:M], pM[:, 0:FT * half].rearrange("p (t m) -> p t m", m=half)).then_inc(f_xs.sem, 1)

        def l_stats(e, it, f):
            done(e, f_xa, it)
            settle(e, e_hold)
            done(e, f_xs, it)
            settle(e, e_hold)
            for t in range(FT):
                i = e.bn_stats(fst[:, t, :], fx[:, t, :])
            i.then_inc(f_st.sem, 1)
            done(e, f_st, it, 0)
            settle(e, e_hold)
            for t in range(FT):
                i = e.bn_aggr(fmv[:, t, :], fst[:, t, :])
            i.then_inc(f_st.sem, 1)

        def l_chain(e, it):
            t, h, x_ = (fnt[:, n, :] for n in range(3))
            y = frs[:, :]
            k = [0]

            def then(i):
                i.then_inc(f_rs.sem, 1)
                k[0] += 1

            def before():
                done(e, f_rs, it, k[0] - 1)

            done(e, f_st, it, 1)
            then(e.tensor_scalar(x_, fmv[:, :, 1], EPS, None, ALU.add))
            yield
            before()
            then(e.tensor_scalar(t.bitcast(I32), x_.bitcast(I32), 1, None, ALU.arith_shift_right))
            yield
            before()
            then(e.tensor_scalar(y.bitcast(I32), t.bitcast(I32), -1.0, float(0x5F3759DF), ALU.mult, ALU.add))
            then(e.tensor_scalar(h, x_, -0.5, None, ALU.mult))
            yield
            for _ in range(NEWTON):
                before()
                then(e.tensor_tensor(t, y, y, ALU.mult))
                yield
                before()
                then(e.tensor_tensor(t, t, h, ALU.mult))
                yield
                before()
                then(e.scalar_tensor_tensor(y, t, 1.5, y, ALU.add, ALU.mult))
                yield

        def l_norm(e, it):
            done(e, f_rs, it, FNORM - 1)
            free(e, f_lt, it, 0, 1)
            for t in range(FT):
                i = e.tensor_scalar(fln[:, t, :], fx[:, t, :], fmv[:, t, 0:1], frs[:, t:t + 1],
                                    ALU.subtract, ALU.mult)
            i.then_inc(f_ln.sem, 1)

        def l_bias(e, it, f):
            done(e, f_sh, it)
            settle(e, e_hold)
            done(e, f_xa, it)
            settle(e, e_hold)
            xd = xr[:, tiles(f), :]
            e.tensor_tensor(xd, xd, b2b[:, :, :].to_broadcast([P, FT, M]), ALU.add).then_inc(f_xb.sem, 1)

        def l_turn(e, it):
            done(e, f_ln, it)
            free(e, f_xn, it, 0, 1)
            for t in range(FT):
                i = e.transpose(pT[:, t * P:(t + 1) * P], fln[:, t, :], ident)
            i.then_inc(f_lt.sem, 1)

        def l_scale(e, it):
            done(e, f_lt, it)
            free(e, f_h, it, 2, 3)
            e.tensor_scalar(xnT, pT[:, :], lng[:, 0:1], lnb[:, 0:1], ALU.mult, ALU.add)\
             .then_inc(f_xn.sem, 1)

        def m_hidden(e, it, n):
            k = FCH[n]
            if n == 0:
                done(e, f_xn, it)
            done(e, f_G, it, (-1, -2, 0)[n])
            for h, bk in ((1, pS), (0, pQ)):
                i = e.matmul(bk[n % 2][0:k, :], w1[:, h * F + n * P:h * F + n * P + k], xnT,
                             start=True, stop=True)
            i.then_inc(f_h.sem, 1)

        def m_warm(e):
            e.activation(warm[:, 1:2], warm[:, 0:1], ACT.Gelu)

        def m_gelu(e, it, n):
            k = FCH[n]
            done(e, f_h, it, n)
            done(e, f_G, it, n - 2 if n else -1)
            e.activation(gel[0:k, n % 2, :], pS[n % 2][0:k, :], ACT.Gelu, bias=b1c[0:k, 1, n:n + 1])\
             .then_inc(f_ge.sem, 1)

        def m_gate(e, it, n):
            k = FCH[n]
            done(e, f_ge, it, n)
            free(e, f_y, it, n, 3)
            e.scalar_tensor_tensor(gT[0:k, n, :], pQ[n % 2][0:k, :], b1c[0:k, 0, n:n + 1], gel[0:k, n % 2, :],
                                   ALU.add, ALU.mult).then_inc(f_G.sem, 1)

        def m_out(e, it, n):
            k = FCH[n]
            done(e, f_G, it, n)
            if n == 0:
                free(e, f_x, it, 0, 1)
            for t in range(FT):
                i = e.matmul(pO[:, t * P:(t + 1) * P], gT[0:k, n, t * P:(t + 1) * P], w2[0:k, n, :],
                             start=(n == 0 and t == 0), stop=(n == 2), skip_group_check=True)
            i.then_inc(f_y.sem, 1)

        def m_add(e, it, f):
            done(e, f_xb, it)
            done(e, f_y, it, 2)
            xd = xr[:, tiles(f), :]
            e.tensor_tensor(xd, pO[:, :].rearrange("p (t m) -> p t m", t=FT), xd, ALU.add).then_inc(f_x.sem, 1)

        def f_slot(en, e, it, f, M_, L_):
            steps = []
            m = lambda fn, *a: steps.append((M_, fn, a))
            n_ = lambda fn, *a: steps.append((L_, fn, a))
            nx = it + 1
            if en == "pe":
                n_(l_shift, nx, f + 1)
                m(m_hidden, it, 0)
                m(m_hidden, it, 1)
                m(m_out, it, 0)
                m(m_hidden, it, 2)
                m(m_out, it, 1)
                n_(l_turn, nx)
                m(m_out, it, 2)
            if en == "act":
                m(m_warm)
                for n in range(3):
                    m(m_gelu, it, n)
            if en == "dve":
                chain = l_chain(e, nx)
                link = lambda *a: next(chain, None)
                n_(l_second, nx)
                n_(l_stats, nx, f + 1)
                n_(link)
                m(m_gate, it, 0)
                for _ in range(5):
                    n_(link)
                m(m_gate, it, 1)
                for _ in range(7):
                    n_(link)
                n_(l_norm, nx)
                m(m_gate, it, 2)
                n_(l_scale, nx)
                m(m_add, it, f)
            if en == "pool":
                n_(l_first, nx, f + 1)
                n_(l_bias, nx, f + 1)
            for on, fn, a in steps:
                if on:
                    fn(e, *a)

        def b_feed_forward(en, e, l):
            f_slot(en, e, l * FP - 1, -1, False, True)
            with e.Fori(0, FP - 1) as f:
                f_slot(en, e, l * FP + f, f, True, True)
            f_slot(en, e, l * FP + (FP - 1), FP - 1, True, False)

        def run(en, e):
            done(e, e_set, 0)
            if en == "pe":
                e.transpose(pM[:, 0:B], cr[:, :], eye[0:B, 0, 0:B]).then_inc(a_cT.sem, 1)
            if en == "act":
                done(e, a_cT, 0)
                e.activation(cT[:, 1, :], pM[:, 0:B], ACT.Exp, scale=-1.0)
                e.copy(cT[:, 0, :], pM[:, 0:B]).then_inc(a_e.sem, 1)
            if en == "dve":
                done(e, a_e, 0)
                e.tensor_scalar(cT[:, 1, :], cT[:, 1, :], 1.0, None, ALU.add).then_inc(a_si.sem, 1)
                done(e, a_si, 0, 0)
                e.reciprocal(cT[:, 2, :], cT[:, 1, :]).then_inc(a_si.sem, 1)
                done(e, a_si, 0, 1)
                e.tensor_tensor(cT[:, 3, :], cT[:, 0, :], cT[:, 2, :], ALU.mult).then_inc(a_si.sem, 1)
            barrier(e, 0)
            with e.Fori(0, B) as b:
                a_pass(en, e, b)
            barrier(e, 1)
            with e.Fori(0, DEPTH) as l:
                done(e, e_wq, l)
                if en == "dve":
                    e.tensor_tensor(rope[:, :, :, :], ropeB[:, :, :, :],
                                    qks[:, :, :].unsqueeze(1).to_broadcast([P, NT, 4, DB]), ALU.mult)\
                     .then_inc(b_rp.sem, 1)
                    done(e, b_rp, l)
                    settle(e, e_hold)
                b_attention(en, e, l)
                barrier(e, l * 2 + 2)
                done(e, e_w1, l)
                settle(e, e_hold)
                b_feed_forward(en, e, l)
                barrier(e, l * 2 + 3)
            if en == "dve":
                for b0 in range(0, 2):
                    lo, hi = b0 * B // 2, (b0 + 1) * B // 2
                    y = xr[:, lo * NT:hi * NT, :].rearrange("p (b t) m -> p b t m", t=NT)
                    e.tensor_tensor(y, y, gb[:, lo:hi, :].unsqueeze(2).to_broadcast([P, B // 2, NT, M]),
                                    ALU.mult).then_inc(o_m.sem, 1)
                done(e, o_m, 0, 1)
                e.tensor_tensor(x1[:, :, :], x1[:, :, :], xr[:, :, :], ALU.add).then_inc(o_m.sem, 1)

        def load_layer_attention(e, l):
            row = lambda a, n: a[bass.ds(l, 1), n].to_broadcast([P, n.stop - n.start])
            lo, hi, full = slice(0, DB // 2), slice(DB // 2, DB), slice(0, DB)
            e.dma_start(wqkvB[:, :, :], Wqkv[bass.ds(l, 1), :, :].rearrange("o m (n c) -> (o m) n c", n=3))\
             .then_inc(e_wq.sem, 16)
            e.dma_start(woB[:, :, :], Wo[bass.ds(l, 1), :, :].rearrange("o (k p) m -> p (o k) m", p=P))\
             .then_inc(e_wq.sem, 16)
            for n, a in enumerate((q_scale, k_scale)):
                e.dma_start(qks[:, 2 * n, full], row(a, full)).then_inc(e_wq.sem, 16)
                e.dma_start(qks[:, 2 * n + 1, lo], row(a, hi)).then_inc(e_wq.sem, 16)
                e.dma_start(qks[:, 2 * n + 1, hi], row(a, lo)).then_inc(e_wq.sem, 16)

        def load_layer_feed_forward(e, l):
            e.dma_start(w1[:, :], W1[bass.ds(l, 1), :, :].rearrange("o m f -> (o m) f")).then_inc(e_w1.sem, 16)
            for n in range(3):
                k = min(P, F - n * P)
                e.dma_start(w2[0:k, n, :], W2[bass.ds(l, 1), n * P:n * P + k, :].rearrange("o f m -> (o f) m"))\
                 .then_inc(e_w1.sem, 16)
            for n, k in enumerate(FCH):
                for h in range(2):
                    lo = h * F + n * P
                    e.dma_start(b1c[0:k, h, n:n + 1], b1[bass.ds(l, 1), lo:lo + k].rearrange("o f -> f o"))\
                     .then_inc(e_w1.sem, 16)
            e.dma_start(b2b[:, 0, :], b2[bass.ds(l, 1), :].to_broadcast([P, M])).then_inc(e_w1.sem, 16)
            e.dma_start(lng[:, :], ln_g[bass.ds(l, 1), :].rearrange("o m -> m o")).then_inc(e_w1.sem, 16)
            e.dma_start(lnb[:, :], ln_b[bass.ds(l, 1), :].rearrange("o m -> m o")).then_inc(e_w1.sem, 16)

        @block.sync
        def _(e):
            for x_ in events:
                if x_.credit:
                    e.sem_inc(x_.sem, x_.credit)
            e.dma_start(x0[:, :, :], x.rearrange("b (t p) m -> p (b t) m", p=P)).then_inc(e_const.sem, 16)
            for n, w in enumerate((wq, wk, wv)):
                e.dma_start(wqkvA[:, n, :], w.rearrange("m h d -> m (h d)")).then_inc(e_const.sem, 16)
            e.dma_start(woA[:, :, :], wo.rearrange("h d m -> d h m")).then_inc(e_const.sem, 16)
            for dst, src in ((ropeA[:, :, :, :], ropeA_in), (ropeB[:, :, :, :], ropeB_in), (eye[:, :, :], eye_in),
                             (mask_f[:, :, :], masks_in), (cr[:, :], c), (wm[:, :], wmod)):
                e.dma_start(dst, src).then_inc(e_const.sem, 16)
            with e.Fori(0, DEPTH) as l:
                e.wait_ge(e_bar.sem, l * 8 + 4)
                settle(e, e_hold)
                load_layer_attention(e, l)
                e.wait_ge(e_bar.sem, l * 8 + 8)
                settle(e, e_hold)
                load_layer_feed_forward(e, l)
                with e.Fori(0, B) as b:
                    for g in range(GROUPS):
                        move_values(e, l * B + b, g)
            done(e, o_m, 0, 2)
            e.dma_start(out.rearrange("b (t p) m -> p (b t) m", p=P), x1[:, :, :]).then_inc(o_out.sem, 16)
            done(e, o_out, 0)

        @block.gpsimd
        def _(e):
            run("pool", e)

        @block.vector
        def _(e):
            e.memset(xsT[64:P, 0:1], 0.0)
            e.memset(warm[:, :], 0.0)
            e.memset(pt[:, :, :, :, :, :], 0.0)
            for g in range(GROUPS):
                e.memset(qd[g][:, :, :, :], 0.0)
                e.memset(kT[g][:, :, 0:WIN], 0.0)
                e.memset(vs[g][0:WIN, 0, :], 0.0)
            done(e, e_const, 0)
            e.tensor_copy(ident16[:, :], ident)
            e.tensor_copy(maskA[:, :], mask_f[:, 0, 0:3 * P])
            e.tensor_copy(maskB[:, :], mask_f[:, 1, :]).then_inc(e_set.sem, 1)
            run("dve", e)

        @block.scalar
        def _(e):
            run("act", e)

        @block.tensor
        def _(e):
            run("pe", e)


def tables():
    f = np.float32
    pos = np.arange(T, dtype=f)
    
    freq = np.power(f(10000.0), (-np.arange(half) / f(half)).astype(f)).astype(f)
    rad = (pos[:, None] * freq[None, :]).astype(f)
    c, s = np.cos(rad).astype(f), np.sin(rad).astype(f)
    ropeA = np.stack([np.concatenate([c, c], -1), np.concatenate([-s, s], -1)], 1)
    hb = np.arange(0, DB, 2, dtype=f)
    inv = (f(1.0) / np.power(f(10000.0), hb / f(DB))).astype(f)
    rad = (pos[:, None] * inv[None, :]).astype(f)
    c, s = np.cos(rad).astype(f), np.sin(rad).astype(f)
    base = ((hb + f(0.4 * DB)) / f(1.4 * DB)).astype(f)
    power = ((pos - T // 2) / f(WIN // 2)).astype(f)
    sc = np.power(base[None, :], power[:, None]).astype(f)
    iv = (f(1.0) / sc).astype(f)
    cat = lambda a, b: np.concatenate([a, b], -1)
    ropeB = np.stack([cat(c * sc, c * sc), cat(-s * sc, s * sc), cat(c * iv, c * iv), cat(-s * iv, s * iv)], 1)
    lay = lambda a: np.ascontiguousarray(a.reshape(NT, P, *a.shape[1:]).transpose(1, 0, 2, 3).astype(f))
    q, k = np.arange(P)[:, None], np.arange(P)[None, :]
    diag = np.where(q < k, f(NEG), f(0))
    maskA = np.concatenate([diag, np.zeros((P, P), f), diag, np.zeros((P, P), f)], 1)
    maskB = np.zeros((2, 2, WIN, 2, NW // 2, 2 * WIN), f)
    r, kk = np.arange(WIN)[:, None], np.arange(2 * WIN)[None, :]
    band = np.where((kk < r) | (kk > r + WIN), f(NEG), f(0))
    maskB += band[None, None, :, None, None, :]
    maskB[0, :, :, :, 0, :WIN] = NEG
    masks = np.ascontiguousarray(np.stack([maskA, maskB.reshape(P, CH)], 1).astype(f))
    eye = np.stack([np.eye(P, dtype=f), np.eye(P, k=1, dtype=f), np.eye(P, k=1 - P, dtype=f)], 1)
    return np.ascontiguousarray(eye), masks, lay(ropeA), lay(ropeB)


_INS = ["L0_attn_x", "L0_attn_wq", "L0_attn_wk", "L0_attn_wv", "L0_attn_wo", "L0_ffn_Wqkv", "L0_ffn_q_scale",
        "L0_ffn_k_scale", "L0_ffn_Wo", "L0_ffn_ln_g", "L0_ffn_ln_b", "L0_ffn_W1", "L0_ffn_b1", "L0_ffn_W2",
        "L0_ffn_b2", "L0_c", "L0_wmod"]


def kernel(**inputs):
    import concourse.bacc as bacc
    from concourse.bass_utils import run_bass_kernel_spmd

    nc = bacc.Bacc("TRN2", target_bir_lowering=False, num_devices=1)
    arrays = {name: np.ascontiguousarray(inputs[name]) for name in _INS}
    for name, table in zip(("eye", "masks", "rope_a", "rope_b"), tables()):
        arrays[name] = table
    args = []
    for name, a in arrays.items():
        args.append(nc.dram_tensor(f"in_{name}", a.shape, mybir.dt.from_np(a.dtype), kind="ExternalInput").ap())
    args.append(nc.dram_tensor("out_0", (B, T, M), F32, kind="ExternalOutput").ap())
    build(nc, *args)
    r = run_bass_kernel_spmd(nc, [{f"in_{n}": a for n, a in arrays.items()}], core_ids=[0])
    return r.results[0]["out_0"]
```

```python
from contextlib import ExitStack

import numpy as np

import concourse.bass as bass
from concourse import mybir

F32 = mybir.dt.float32
BF16 = mybir.dt.bfloat16
F32R = mybir.dt.float32r
ACT = mybir.ActivationFunctionType
ALU = mybir.AluOpType
AX = mybir.AxisListType

P = 128
B, T, M = 8, 256, 128
NT = T // P
CH = 512
INNER = 1024
GROUPS = INNER // CH
DEPTH, HB, DB, WIN = 6, 16, 64, 32
NW = T // WIN
HA, DA = 8, 128
F = int(M * 4 * 2 / 3)
FCH = [min(P, F - n) for n in range(0, F, P)]
HALF = M // 2
FT = CH // P
FP = B * NT // FT
NEG = -1.0e30
QK = GROUPS * NT * 2
NCH = GROUPS * NT * 3
UNITS = 4
PAIRS = HB // 2
EPS = 1e-5
NEWTON = 3
I32 = mybir.dt.int32
FNORM = 4 + 3 * NEWTON
NORM = 4 + 3 * NEWTON


class Ev:

    def __init__(self, sem, per, credit=0, step=1):
        self.sem, self.per, self.credit, self.step = sem, per, credit, step

    def value(self, it, k):
        return it * (self.per * self.step) + (self.credit + (k + 1) * self.step)


def done(eng, ev, it, k=0):
    v = ev.value(it, k)
    if isinstance(v, int) and v <= ev.credit:
        return
    eng.wait_ge(ev.sem, v)


def settle(eng, ev):
    eng.sem_inc(ev.sem, 1)


def free(eng, ev, it, k, ring):
    done(eng, ev, it, k - ring)


def build(nc, x, wq, wk, wv, wo, Wqkv, q_scale, k_scale, Wo, ln_g, ln_b, W1, b1, W2, b2, c, wmod,
          eye_in, masks_in, ropeA_in, ropeB_in, out):
    with ExitStack() as ctx:
        def sb(name, shape, dt=F32):
            return ctx.enter_context(nc.sbuf_tensor(name, shape, dt))

        def ev(name, per, credit=0, step=1):
            e = Ev(ctx.enter_context(nc.semaphore(name)), per, credit, step)
            events.append(e)
            return e

        events = []
        eye = sb("eye", [P, 3, P])
        ident, down, wrap = (eye[:, n, :] for n in range(3))
        ident16 = sb("ident16", [P, P], BF16)
        maskA = sb("maskA", [P, 3 * P], BF16)
        maskB = sb("maskB", [P, CH], BF16)
        ropeA = sb("ropeA", [P, NT, 2, DA])
        ropeB = sb("ropeB", [P, NT, 4, DB])
        rope = sb("rope", [P, NT, 4, DB])
        qks = sb("qks", [P, 4, DB])
        wqkvA = sb("wqkvA", [P, 3, INNER])
        woA = sb("woA", [P, HA, M])
        wqkvB = wqkvA
        w_high = sb("w_high", [P, 3, INNER], F32R)
        w_low = sb("w_low", [P, 3, INNER], F32R)
        woB = sb("woB", [P, PAIRS, M])
        w1 = sb("w1", [P, 2 * F])
        w2 = sb("w2", [P, 3, M])
        b1c = sb("b1c", [P, 2, len(FCH)])
        b2b = sb("b2b", [P, 1, M])
        lng = sb("lng", [P, 1])
        lnb = sb("lnb", [P, 1])
        x0 = sb("x0", [P, B * NT, M])
        x1 = sb("x1", [P, B * NT, M])
        xr = sb("xr", [P, B * NT, M])
        gb = sb("gb", [P, B, M])
        wm = sb("wm", [P, 6 * M])
        cr = sb("cr", [B, M])
        cT = sb("cT", [P, 4, B])
        cb = sb("cb", [P, P])
        s1T = sb("s1T", [P, B, 2])
        s1 = sb("s1", [P, 2])
        mod = sb("mod", [P, 4, M])
        gate = sb("gate", [P, 2, M])
        ga = sb("ga", [P, 2, M])
        stat = sb("stat", [P, NT, 6])
        mv = sb("mv", [P, NT, 2])
        rstd = sb("rstd", [P, NT])
        st1 = sb("st1", [P, NT, 6])
        mv1 = sb("mv1", [P, NT, 2])
        rstd1 = sb("rstd1", [P, NT])
        n1 = sb("n1", [P, 3, NT])
        n2 = sb("n2", [P, 3, NT])
        ln1 = sb("ln1", [P, NT, M])
        nt = sb("nt", [P, 2, 32])
        ln = sb("ln", [P, NT, M])
        xcur = sb("xcur", [P, NT, M])
        hT = sb("hT", [P, T])
        xsh = sb("xsh", [P, T], F32R)
        xsl = sb("xsl", [P, T], F32R)
        sq = sb("sq", [P, 2, CH])
        ra = sb("ra", [P, 4, CH])
        rb = sb("rb", [P, 2, CH])
        qn = sb("qn", [P, 4, CH])
        ss = sb("ss", [P, 4, 8])
        sx = sb("sx", [P, 32])
        rs = sb("rs", [P, 4, 8])
        v = [sb(f"v{g}", [P, NT, CH]) for g in range(GROUPS)]
        vs = [sb(f"vs{g}", [P, NT, CH]) for g in range(GROUPS)]
        qd = [sb(f"qd{g}", [P, 4, NW, 2 * WIN]) for g in range(GROUPS)]
        kT = [sb(f"kT{g}", [P, 4, WIN + T]) for g in range(GROUPS)]
        qT = [a[:, :, :, :].rearrange("p h w q -> p (h w q)")[:, 0:4 * T].rearrange("p (h t) -> p h t", h=4)
              for a in qd]
        dif = sb("dif", [P, 2, CH])
        mask_f = dif
        pr = sb("pr", [P, 2, CH])
        mx = sb("mx", [P, 2, 8])
        sm = sb("sm", [P, 2, 8])
        rl = sb("rl", [P, 2, 8])
        pt = sb("pt", [P, 2, 4, 2, 2, 2 * WIN])
        ptA = sb("ptA", [P, 2, 3 * P])
        oT = sb("oT", [P, PAIRS, T])
        warm = sb("warm", [1, 2])
        fst = sb("fst", [P, FT, 6])
        fmv = sb("fmv", [P, FT, 2])
        frs = sb("frs", [P, FT])
        fnt = sb("fnt", [P, 3, FT])
        fln = qn[:, 0, :].rearrange("p (t m) -> p t m", t=FT)
        xnT = qn[:, 1, :]
        gel = rb
        fx = sb("fx", [P, FT, M])
        gT = ra
        yo = sb("yo", [P, NT, M])

        def bank(name):
            return ctx.enter_context(nc.psum_tensor(name, [P, CH], F32))

        pQ = [bank("pQ0"), bank("pQ1")]
        pT = bank("pT")
        pS = [bank("pS0"), bank("pS1")]
        pP = bank("pP")
        pO = bank("pO")
        pM = bank("pM")
        pV = [pO, pM]

        e_const = ev("e_const", 1, step=16 * 11)
        e_set = ev("e_set", 1)
        e_hold = ev("e_hold", 1)
        e_bar = ev("e_bar", 1)
        a_cT = ev("a_cT", 1)
        a_e = ev("a_e", 1)
        a_si = ev("a_si", 3)
        a_mt = ev("a_mt", 1)
        a_m1 = ev("a_m1", 1)
        a_st = ev("a_st", 2)
        a_r1 = ev("a_r1", FNORM)
        a_ln = ev("a_ln", 1)
        a_hT = ev("a_hT", 1, 1)
        a_hc = ev("a_hc", 1, 1)
        a_pj = ev("a_pj", NCH, NCH)
        a_ev = ev("a_ev", GROUPS * NT, 2)
        a_ab = ev("a_ab", QK, 2)
        a_qn = ev("a_qn", QK, 2)
        a_tr = ev("a_tr", QK, 4)
        a_tc = ev("a_tc", QK, 1)
        a_S = ev("a_S", HA, HA)
        a_mx = ev("a_mx", HA)
        a_nm = ev("a_nm", HA)
        a_ex = ev("a_ex", HA, 2)
        a_rl = ev("a_rl", HA)
        a_pn = ev("a_pn", HA)
        a_pt = ev("a_pt", HA, 2)
        a_pc = ev("a_pc", HA, 1)
        a_pv = ev("a_pv", HA, HA)
        a_oc = ev("a_oc", HA, 2)
        a_wo = ev("a_wo", 1, 1)
        a_cb = ev("a_cb", 1)
        a_mo = ev("a_mo", 1, 1)
        a_mc = ev("a_mc", 1, 1)
        a_g = ev("a_g", 6)
        a_y = ev("a_y", 2, 2)
        a_s2 = ev("a_s2", 2)
        a_r2 = ev("a_r2", FNORM)
        a_l2 = ev("a_l2", 1)
        a_x = ev("a_x", 2, 2)
        e_wq = ev("e_wq", 1, step=16 * 8)
        e_w1 = ev("e_w1", 1, step=16 * 13)
        b_z = ev("b_z", 1)
        b_rp = ev("b_rp", 1)
        b_xc = ev("b_xc", 1)
        b_xt = ev("b_xt", 1, 1)
        b_xh = ev("b_xh", 1)
        b_xs = ev("b_xs", 1)
        b_wh = ev("b_wh", 3 * GROUPS)
        b_wl = ev("b_wl", 1)
        b_pj = ev("b_pj", NCH, NCH)
        b_ev = ev("b_ev", GROUPS * NT, 2)
        b_sq = ev("b_sq", QK)
        b_ss = ev("b_ss", QK, 2)
        b_rs = ev("b_rs", GROUPS * NORM)
        b_ab = ev("b_ab", QK, 2)
        b_ad = ev("b_ad", QK, 2)
        b_qn = ev("b_qn", QK, 4)
        b_tr = ev("b_tr", QK, 4)
        b_tc = ev("b_tc", QK, 2)
        b_vs = [ev(f"b_vs{g}", 1, step=16 * 2) for g in range(GROUPS)]
        b_S = ev("b_S", UNITS, UNITS)
        b_mx = ev("b_mx", UNITS)
        b_sub = ev("b_sub", UNITS, 2)
        b_ex = ev("b_ex", UNITS, 2)
        b_sm = ev("b_sm", UNITS)
        b_rl = ev("b_rl", UNITS)
        b_pn = ev("b_pn", UNITS)
        b_pt = ev("b_pt", UNITS, 2)
        b_pc = ev("b_pc", UNITS, 2)
        b_pv = ev("b_pv", PAIRS, PAIRS)
        b_oc = ev("b_oc", PAIRS, PAIRS + 1)
        b_wo = ev("b_wo", 1, 1)
        b_wx = ev("b_wx", 1, 1)
        f_sh = ev("f_sh", 1)
        f_xa = ev("f_xa", 1)
        f_xs = ev("f_xs", 1, 1)
        f_st = ev("f_st", 2)
        f_rs = ev("f_rs", FNORM, 0)
        f_ln = ev("f_ln", 1, 1)
        f_xb = ev("f_xb", 1)
        f_lt = ev("f_lt", 1, 1)
        f_xn = ev("f_xn", 1, 1)
        f_h = ev("f_h", 3, 3)
        f_ge = ev("f_ge", 3)
        f_G = ev("f_G", 3, 3)
        f_y = ev("f_y", 3, 3)
        f_x = ev("f_x", 1, 1)
        o_m = ev("o_m", 3)
        o_out = ev("o_out", 1, step=16)

        block = ctx.enter_context(nc.Block())

        def barrier(eng, n):
            eng.drain().then_inc(e_bar.sem, 1)
            eng.wait_ge(e_bar.sem, (n + 1) * 4)
            settle(eng, e_hold)

        def rsqrt_chain(e, evt, it, y, var, tmp):
            t, h, x_ = (tmp[:, n, :] for n in range(3))
            k = [0]

            def then(i):
                i.then_inc(evt.sem, 1)
                k[0] += 1

            def before():
                done(e, evt, it, k[0] - 1)

            then(e.tensor_scalar(x_, var, EPS, None, ALU.add))
            yield
            before()
            then(e.tensor_scalar(t.bitcast(I32), x_.bitcast(I32), 1, None, ALU.arith_shift_right))
            yield
            before()
            then(e.tensor_scalar(y.bitcast(I32), t.bitcast(I32), -1.0, float(0x5F3759DF), ALU.mult, ALU.add))
            then(e.tensor_scalar(h, x_, -0.5, None, ALU.mult))
            yield
            for _ in range(NEWTON):
                before()
                then(e.tensor_tensor(t, y, y, ALU.mult))
                yield
                before()
                then(e.tensor_tensor(t, t, h, ALU.mult))
                yield
                before()
                then(e.scalar_tensor_tensor(y, t, 1.5, y, ALU.add, ALU.mult))
                yield

        def moments(e, evt, it, stats, mv_, tiles_):
            settle(e, e_hold)
            for t, x_ in enumerate(tiles_):
                i = e.bn_stats(stats[:, t, :], x_)
            i.then_inc(evt.sem, 1)
            done(e, evt, it, 0)
            settle(e, e_hold)
            for t in range(len(tiles_)):
                i = e.bn_aggr(mv_[:, t, :], stats[:, t, :])
            i.then_inc(evt.sem, 1)

        def chunk_a(c):
            return c // 6, (c % 6) // 3, c % 3

        def chunk(c):
            r = c % 6
            return (c // 6, r // 2, r % 2) if r < 4 else (c // 6, r - 4, 2)

        def bank_read(e, it, c_, order, rotated, moved):
            g, t, kind = order((c_ - 2) % NCH)
            n = g * 2 + t if kind == 2 else g * 4 + t * 2 + kind
            per = GROUPS * NT if kind == 2 else QK
            done(e, moved if kind == 2 else rotated, it, n if c_ >= 2 else n - per)

        tiles2 = lambda a, b: [a[:, bass.ds(b * NT + t, 1), :].rearrange("p o m -> p (o m)") for t in range(NT)]

        def norm1_stats(e, it, b):
            moments(e, a_st, it, st1, mv1, tiles2(x0, b))

        def norm1_chain(e, it):
            done(e, a_st, it, 1)
            yield from rsqrt_chain(e, a_r1, it, rstd1[:, :], mv1[:, :, 1], n1)

        def norm1(e, it, b):
            done(e, a_r1, it, FNORM - 1)
            free(e, a_hT, it, 0, 1)
            for t, x_ in enumerate(tiles2(x0, b)):
                i = e.tensor_scalar(ln1[:, t, :], x_, mv1[:, t, 0:1], rstd1[:, t:t + 1], ALU.subtract, ALU.mult)
            i.then_inc(a_ln.sem, 1)

        def norm1_turn(e, it, first=False):
            done(e, a_ln, it)
            if not first:
                done(e, a_oc, it - 1, 1)
            for t in range(NT):
                i = e.transpose(pM[:, t * P:(t + 1) * P], ln1[:, t, :], ident)
            i.then_inc(a_hT.sem, 1)

        def pick1(e, it, b):
            free(e, a_hc, it, 0, 1)
            settle(e, e_hold)
            e.tensor_copy(s1[:, :], s1T[:, bass.ds(b, 1), :].rearrange("p o n -> p (o n)")).then_inc(a_m1.sem, 1)

        def modulate1(e, it):
            done(e, a_hT, it)
            done(e, a_m1, it)
            free(e, a_pj, it, NCH - 1, NCH)
            e.tensor_scalar(hT[:, :], pM[:, 0:T], s1[:, 0:1], s1[:, 1:2], ALU.mult, ALU.add)\
             .then_inc(a_hc.sem, 1)

        def proj_a(e, it, c_):
            g, t, kind = chunk_a(c_)
            if c_ == 0:
                done(e, a_hc, it)
            bank_read(e, it, c_, chunk_a, a_ab, a_ev)
            e.matmul(pQ[c_ % 2][:, :], hT[:, t * P:(t + 1) * P], wqkvA[:, kind, g * CH:(g + 1) * CH],
                     start=True, stop=True).then_inc(a_pj.sem, 1)

        def move_v_a(e, it, c_):
            g, t, kind = chunk_a(c_)
            done(e, a_pj, it, c_)
            free(e, a_pv, it, 4 * g + 3, HA)
            e.copy(v[g][:, t, :], pQ[c_ % 2][:, :]).then_inc(a_ev.sem, 1)

        def rotate_a(e, it, j):
            g, t, kind = j // 4, (j % 4) // 2, j % 2
            c_ = g * 6 + t * 3 + kind
            done(e, a_pj, it, c_)
            r = pQ[c_ % 2][:, :].rearrange("p (h s d) -> p h s d", s=2, d=DA // 2)
            shape = [P, 4, 2, DA // 2]
            cos, sin = (ropeA[:, t:t + 1, n, :].rearrange("p o (s d) -> p o s d", s=2).to_broadcast(shape)
                        for n in range(2))
            free(e, a_qn, it, j, 2)
            oa, ob = (y[:, j % 2, :].rearrange("p (h s d) -> p h s d", s=2, d=DA // 2) for y in (ra, rb))
            e.tensor_tensor(oa, r, cos, ALU.mult)
            e.tensor_tensor(ob, r[:, :, ::-1, :], sin, ALU.mult).then_inc(a_ab.sem, 1)

        def add_a(e, it, j):
            done(e, a_ab, it, j)
            free(e, a_tr, it, j, 4)
            e.tensor_tensor(qn[:, j % 4, :], ra[:, j % 2, :], rb[:, j % 2, :], ALU.add).then_inc(a_qn.sem, 1)

        def turn_a(e, it, j):
            done(e, a_qn, it, j)
            free(e, a_tc, it, j, 1)
            if j == 4:
                free(e, a_mc, it, 0, 1)
            for h in range(4):
                i = e.transpose(pT[:, h * P:(h + 1) * P], qn[:, j % 4, h * P:(h + 1) * P], ident)
            i.then_inc(a_tr.sem, 1)

        def turn_copy_a(e, it, j):
            g, t, isk = j // 4, (j % 4) // 2, j % 2
            done(e, a_tr, it, j)
            if j % 4 == 0:
                free(e, a_S, it, 4 * g + 3, HA)
            dst = kT[g][:, :, WIN + t * P:WIN + (t + 1) * P] if isk else qT[g][:, :, t * P:(t + 1) * P]
            e.copy(dst, pT[:, :].rearrange("p (h q) -> p h q", h=4)).then_inc(a_tc.sem, 1)

        spans = ((0, P), (P, 3 * P))

        def scores_a(e, it, h):
            g, s = h // 4, h % 2
            done(e, a_tc, it, 4 * g + 3)
            free(e, a_ex, it, h, 2)
            e.matmul(pS[s][:, 0:3 * P], ident16[:, :], maskA[:, :], start=True, stop=False,
                     skip_group_check=True)
            for t, (lo, hi) in enumerate(spans):
                i = e.matmul(pS[s][:, lo:hi], qT[g][:, h % 4, t * P:(t + 1) * P],
                             kT[g][:, h % 4, WIN:WIN + (t + 1) * P], start=False, stop=True,
                             skip_group_check=True)
            i.then_inc(a_S.sem, 1)

        def max_a(e, it, h):
            s = h % 2
            done(e, a_S, it, h)
            free(e, a_ex, it, h, 2)
            for t, (lo, hi) in enumerate(spans):
                i = e.tensor_reduce(mx[:, s, t:t + 1], pS[s][:, lo:hi], AX.X, ALU.max)
            i.then_inc(a_mx.sem, 1)
            done(e, a_mx, it, h)
            e.tensor_scalar(mx[:, s, 2:4], mx[:, s, 0:2], -1.0 / DA, None, ALU.mult).then_inc(a_nm.sem, 1)

        def exponent_a(e, it, h):
            s = h % 2
            done(e, a_nm, it, h)
            free(e, a_pt, it, h, 2)
            for t, (lo, hi) in enumerate(spans):
                i = e.activation(pr[:, s, lo:hi], pS[s][:, lo:hi], ACT.Exp, bias=mx[:, s, 2 + t:3 + t],
                                 scale=1.0 / DA, accum_out=sm[:, s, t:t + 1])
            i.then_inc(a_ex.sem, 1)

        def soft_norm_a(e, it, h):
            s = h % 2
            done(e, a_ex, it, h)
            e.reciprocal(rl[:, s, 0:2], sm[:, s, 0:2]).then_inc(a_rl.sem, 1)
            done(e, a_rl, it, h)
            for t, (lo, hi) in enumerate(spans):
                i = e.tensor_scalar(pr[:, s, lo:hi], pr[:, s, lo:hi], rl[:, s, t:t + 1], None, ALU.mult)
            i.then_inc(a_pn.sem, 1)

        def turn_p_a(e, it, h):
            done(e, a_pn, it, h)
            free(e, a_pc, it, h, 1)
            for n in range(3):
                i = e.transpose(pP[:, n * P:(n + 1) * P], pr[:, h % 2, n * P:(n + 1) * P], ident)
            i.then_inc(a_pt.sem, 1)

        def copy_p_a(e, it, h):
            done(e, a_pt, it, h)
            free(e, a_pv, it, h, 2)
            e.copy(ptA[:, h % 2, :], pP[:, 0:3 * P]).then_inc(a_pc.sem, 1)

        def values_a(e, it, h, *shared):
            g, s = h // 4, h % 2
            done(e, a_pc, it, h)
            if h % 4 == 0:
                done(e, a_ev, it, 2 * g + 1)
            free(e, a_oc, it, h, 2)
            if shared:
                done(e, *shared)
            for q, k, n in ((0, 0, 0), (1, 0, 1), (1, 1, 2)):
                i = e.matmul(pV[s][:, q * P:(q + 1) * P], v[g][:, k, (h % 4) * P:(h % 4 + 1) * P],
                             ptA[:, s, n * P:(n + 1) * P], start=(k == 0), stop=(k == q))
            i.then_inc(a_pv.sem, 1)

        def copy_o_a(e, it, h):
            done(e, a_pv, it, h)
            if h == 0:
                free(e, a_wo, it, 0, 1)
            e.copy(oT[:, h, :], pV[h % 2][:, 0:T]).then_inc(a_oc.sem, 1)

        def spread(e, it, b):
            free(e, a_mo, it, 0, 1)
            settle(e, e_hold)
            e.tensor_copy(cb[:, :], cT[:, 3, bass.ds(b, 1)].to_broadcast([P, P])).then_inc(a_cb.sem, 1)

        def modulation(e, it, turned):
            done(e, a_cb, it)
            done(e, a_tc, *turned)
            e.matmul(pT[:, :], cb[:, :], wm[:, 2 * M:6 * M], start=True, stop=True).then_inc(a_mo.sem, 1)

        def modulation_copy(e, it):
            done(e, a_mo, it)
            free(e, a_x, it, 1, 2)
            e.copy(mod[:, :, :], pT[:, :].rearrange("p (n m) -> p n m", n=4)).then_inc(a_mc.sem, 1)

        def gates(e, it, b):
            done(e, a_mc, it)
            free(e, a_y, it, 0, 2)
            g3 = mod[:, 0::3, :]
            e.tensor_scalar(gate[:, :, :], g3, 0.0, 2.0, ALU.is_ge, ALU.mult).then_inc(a_g.sem, 1)
            e.scalar_tensor_tensor(ga[:, :, :], g3, -1.0, g3, ALU.mult, ALU.max).then_inc(a_g.sem, 1)
            done(e, a_g, it, 0)
            e.tensor_scalar(gate[:, :, :], gate[:, :, :], -1.0, None, ALU.add).then_inc(a_g.sem, 1)
            e.tensor_scalar(mod[:, 2, :], mod[:, 2, :], 1.0, None, ALU.add).then_inc(a_g.sem, 1)
            done(e, a_g, it, 2)
            e.scalar_tensor_tensor(gate[:, :, :], ga[:, :, :], 0.25, gate[:, :, :], ALU.max, ALU.mult)\
             .then_inc(a_g.sem, 1)
            done(e, a_g, it, 4)
            e.tensor_copy(gb[:, bass.ds(b, 1), :], gate[:, 1:2, :]).then_inc(a_g.sem, 1)

        def out_a(e, it):
            done(e, a_oc, it, HA - 1)
            for t in range(NT):
                for h in range(HA):
                    i = e.matmul(pO[:, t * M:(t + 1) * M], oT[:, h, t * P:(t + 1) * P], woA[:, h, :],
                                 start=(h == 0), stop=(h == HA - 1))
            i.then_inc(a_wo.sem, 1)

        def residual_a(e, it, b):
            done(e, a_wo, it)
            done(e, a_g, it, 4)
            e.tensor_tensor(yo[:, :, :], pO[:, 0:T].rearrange("p (t m) -> p t m", t=NT),
                            gate[:, 0:1, :].to_broadcast([P, NT, M]), ALU.mult).then_inc(a_y.sem, 1)
            done(e, a_y, it, 0)
            e.tensor_tensor(x1[:, bass.ds(b * NT, NT), :], x0[:, bass.ds(b * NT, NT), :], yo[:, :, :], ALU.add)\
             .then_inc(a_y.sem, 1)
            done(e, a_y, it, 1)
            moments(e, a_s2, it, stat, mv, tiles2(x1, b))

        def norm2_chain(e, it):
            done(e, a_s2, it, 1)
            yield from rsqrt_chain(e, a_r2, it, rstd[:, :], mv[:, :, 1], n2)

        def norm2(e, it, b):
            done(e, a_r2, it, FNORM - 1)
            free(e, a_x, it, 0, 2)
            for t, x_ in enumerate(tiles2(x1, b)):
                i = e.tensor_scalar(ln[:, t, :], x_, mv[:, t, 0:1], rstd[:, t:t + 1], ALU.subtract, ALU.mult)
            i.then_inc(a_l2.sem, 1)

        def modulate2(e, it, b):
            done(e, a_l2, it)
            done(e, a_g, it, 3)
            free(e, a_x, it, 1, 2)
            e.tensor_tensor(ln[:, :, :], ln[:, :, :], mod[:, 2:3, :].to_broadcast([P, NT, M]), ALU.mult)\
             .then_inc(a_x.sem, 1)
            done(e, a_x, it, 0)
            settle(e, e_hold)
            e.tensor_tensor(xr[:, bass.ds(b * NT, NT), :], ln[:, :, :], mod[:, 1:2, :].to_broadcast([P, NT, M]),
                            ALU.add).then_inc(a_x.sem, 1)

        def slot_a(en, e, it, b, g, F_, K_, L_, nxt=False):
            ib, gb_ = (it, g - 1) if g else (it - 1, GROUPS - 1)
            il, gl = it - 1, g
            c0, j0 = 6 * g, 4 * g
            jb, h0 = 4 * gb_, 4 * gb_
            hl = 4 * gl + 3
            steps = []
            F = lambda f, *a, on=True: steps.append((F_ and on, f, a))
            K = lambda f, *a, on=True: steps.append((K_ and on, f, a))
            L = lambda f, *a, on=True: steps.append((L_ and on, f, a))
            first, second = g == 0, g == 1
            if en == "pe":
                L(turn_p_a, il, hl)
                F(proj_a, it, c0)
                K(turn_a, ib, jb)
                F(proj_a, it, c0 + 1)
                K(turn_a, ib, jb + 1)
                L(values_a, il, hl, *((a_hc, it) if first and F_ else ()))
                K(turn_a, ib, jb + 2)
                F(proj_a, it, c0 + 2)
                K(turn_a, ib, jb + 3)
                L(out_a, il, on=second)
                K(scores_a, ib, h0)
                F(proj_a, it, c0 + 3)
                K(scores_a, ib, h0 + 1)
                L(modulation, il, (it, 3) if K_ else (il, 7), on=second)
                F(proj_a, it, c0 + 4)
                K(turn_p_a, ib, h0)
                K(scores_a, ib, h0 + 2)
                K(values_a, ib, h0, *((a_y, il, 0) if second and L_ else ()))
                K(turn_p_a, ib, h0 + 1)
                K(scores_a, ib, h0 + 3)
                F(proj_a, it, c0 + 5)
                K(values_a, ib, h0 + 1)
                K(turn_p_a, ib, h0 + 2)
                F(norm1_turn, it + 1, on=second and nxt)
                K(values_a, ib, h0 + 2)
            if en == "act":
                K(turn_copy_a, ib, jb)
                L(copy_p_a, il, hl)
                K(turn_copy_a, ib, jb + 1)
                L(copy_o_a, il, hl)
                K(turn_copy_a, ib, jb + 2)
                F(move_v_a, it, c0 + 2)
                K(turn_copy_a, ib, jb + 3)
                K(exponent_a, ib, h0)
                L(modulation_copy, il, on=second)
                K(exponent_a, ib, h0 + 1)
                K(copy_p_a, ib, h0)
                K(exponent_a, ib, h0 + 2)
                K(copy_p_a, ib, h0 + 1)
                K(copy_o_a, ib, h0)
                K(exponent_a, ib, h0 + 3)
                K(copy_p_a, ib, h0 + 2)
                K(copy_o_a, ib, h0 + 1)
                F(move_v_a, it, c0 + 5)
                K(copy_o_a, ib, h0 + 2)
            if en == "dve":
                ln_on = nxt and first
                chain = norm1_chain(e, it + 1) if first else norm2_chain(e, il)
                link = lambda *a: next(chain, None)

                def links(n):
                    for _ in range(n):
                        F(link, on=first and nxt)

                def links2(n):
                    for _ in range(n):
                        L(link, on=second)

                F(rotate_a, it, j0)
                F(norm1_stats, it + 1, b + 1, on=ln_on)
                F(rotate_a, it, j0 + 1)
                K(max_a, ib, h0)
                F(rotate_a, it, j0 + 2)
                K(max_a, ib, h0 + 1)
                K(soft_norm_a, ib, h0)
                L(gates, il, b - 1, on=second)
                L(residual_a, il, b - 1, on=second)
                links(1)
                links2(1)
                K(soft_norm_a, ib, h0 + 1)
                links(3)
                links2(2)
                K(max_a, ib, h0 + 2)
                links(2)
                links2(3)
                F(rotate_a, it, j0 + 3)
                links(1)
                links2(1)
                K(max_a, ib, h0 + 3)
                links(3)
                links2(2)
                K(soft_norm_a, ib, h0 + 2)
                links(3)
                links2(2)
                F(norm1, it + 1, b + 1, on=ln_on)
                links2(2)
                L(norm2, il, b - 1, on=second)
                K(soft_norm_a, ib, h0 + 3)
                F(modulate1, it + 1, on=second and nxt)
            if en == "pool":
                L(spread, il, b - 1, on=second)
                F(add_a, it, j0)
                F(add_a, it, j0 + 1)
                F(pick1, it + 1, b + 1, on=second and nxt)
                L(modulate2, il, b - 1, on=second)
                F(add_a, it, j0 + 2)
                F(add_a, it, j0 + 3)
            for on, f, a in steps:
                if on:
                    f(e, *a)

        def part_a(en, e):
            if en == "pool":
                pick1(e, 0, 0)
            if en == "dve":
                norm1_stats(e, 0, 0)
                for _ in norm1_chain(e, 0):
                    pass
                norm1(e, 0, 0)
                modulate1(e, 0)
            if en == "pe":
                norm1_turn(e, 0, first=True)
            slot_a(en, e, 0, 0, 0, True, False, False, True)
            slot_a(en, e, 0, 0, 1, True, True, False, True)
            with e.Fori(1, B - 1) as b:
                slot_a(en, e, b, b, 0, True, True, True, True)
                slot_a(en, e, b, b, 1, True, True, True, True)
            slot_a(en, e, B - 1, B - 1, 0, True, True, True)
            slot_a(en, e, B - 1, B - 1, 1, True, True, True)
            slot_a(en, e, B, B, 0, False, True, True)
            split_weights(en, e, 0)
            slot_a(en, e, B, B, 1, False, False, True)


        def xt_copy(e, it, b):
            free(e, b_xt, it, 0, 1)
            settle(e, e_hold)
            e.tensor_copy(xcur[:, :, :], xr[:, bass.ds(b * NT, NT), :]).then_inc(b_xc.sem, 1)

        def xt_turn(e, it):
            done(e, b_xc, it)
            done(e, b_oc, it - 2, PAIRS - 1)
            for t in range(NT):
                i = e.transpose(pM[:, t * M:(t + 1) * M], xcur[:, t, :], ident)
            i.then_inc(b_xt.sem, 1)

        shifted = ((slice(0, HALF), slice(0, T), slice(0, T)), (slice(HALF, P), slice(1, T), slice(0, T - 1)))

        def xt_shift(e, it):
            done(e, b_xt, it)
            free(e, b_pj, it, NCH - 1, NCH)
            for p, to, fr in shifted:
                i = e.copy(xsh[p, to], pM[p, fr])
            i.then_inc(b_xh.sem, 1)

        def xt_low(e, it):
            done(e, b_xh, it)
            for p, to, fr in shifted:
                i = e.tensor_tensor(xsl[p, to], pM[p, fr], xsh[p, to].bitcast(F32), ALU.subtract)
            i.then_inc(b_xs.sem, 1)

        def split_weights(en, e, l):
            if en == "act":
                done(e, e_wq, l)
                settle(e, e_hold)
                for n in range(3):
                    for g in range(GROUPS):
                        c_ = slice(g * CH, (g + 1) * CH)
                        e.copy(w_high[:, n, c_], wqkvB[:, n, c_]).then_inc(b_wh.sem, 1)
            if en == "pool":
                for n in range(3):
                    for g in range(GROUPS):
                        c_ = slice(g * CH, (g + 1) * CH)
                        done(e, b_wh, l, n * GROUPS + g)
                        i = e.tensor_tensor(w_low[:, n, c_], wqkvB[:, n, c_], w_high[:, n, c_].bitcast(F32),
                                            ALU.subtract)
                i.then_inc(b_wl.sem, 1)

        def proj(e, it, c_):
            g, t, kind = chunk(c_)
            if c_ == 0:
                done(e, b_xs, it)
            bank_read(e, it, c_, chunk, b_ab, b_ev)
            for n, (x_, w) in enumerate(((xsh, w_high), (xsh, w_low), (xsl, w_high))):
                i = e.matmul(pQ[c_ % 2][:, :], x_[:, t * P:(t + 1) * P], w[:, kind, g * CH:(g + 1) * CH],
                             start=(n == 0), stop=(n == 2))
            i.then_inc(b_pj.sem, 1)

        def square(e, it, j):
            g, t, kind = j // 4, (j % 4) // 2, j % 2
            c_ = g * 6 + j % 4
            done(e, b_pj, it, c_)
            free(e, b_ss, it, j, 2)
            e.activation(sq[:, j % 2, :], pQ[c_ % 2][:, :], ACT.Square).then_inc(b_sq.sem, 1)

        def move_v(e, it, c_):
            g, t, kind = chunk(c_)
            done(e, b_pj, it, c_)
            free(e, b_pv, it, 4 * g + 3, PAIRS)
            e.copy(v[g][:, t, :], pQ[c_ % 2][:, :]).then_inc(b_ev.sem, 1)

        def rotate(e, it, j):
            g, t, kind = j // 4, (j % 4) // 2, j % 2
            c_ = g * 6 + j % 4
            done(e, b_sq, it, j)
            e.tensor_reduce(ss[:, j % 4, :], sq[:, j % 2, :].rearrange("p (h d) -> p h d", d=DB),
                            AX.X, ALU.add).then_inc(b_ss.sem, 1)
            free(e, b_ad, it, j, 2)
            free(e, b_qn, it, j, 4)
            r = pQ[c_ % 2][:, :].rearrange("p (h s d) -> p h s d", s=2, d=DB // 2)
            shape = [P, 8, 2, DB // 2]
            cos, sin = (rope[:, t:t + 1, 2 * kind + n, :].rearrange("p o (s d) -> p o s d", s=2)
                        .to_broadcast(shape) for n in range(2))
            oa, ob = (y.rearrange("p (h s d) -> p h s d", s=2, d=DB // 2)
                      for y in (ra[:, j % 4, :], rb[:, j % 2, :]))
            e.tensor_tensor(oa, r, cos, ALU.mult)
            e.tensor_tensor(ob, r[:, :, ::-1, :], sin, ALU.mult).then_inc(b_ab.sem, 1)

        def rotate_add(e, it, j):
            done(e, b_ab, it, j)
            e.tensor_tensor(ra[:, j % 4, :], ra[:, j % 4, :], rb[:, j % 2, :], ALU.add).then_inc(b_ad.sem, 1)

        flat = lambda y: y.rearrange("p n h -> p (n h)")
        x_, y_ = flat(ss[:, :, :]), flat(rs[:, :, :])

        def norm_chain(e, it, g):
            k = [g * NORM]

            def then(i):
                i.then_inc(b_rs.sem, 1)
                k[0] += 1

            def before():
                done(e, b_rs, it, k[0] - 1)

            t, h = nt[:, 0, :], nt[:, 1, :]
            done(e, b_ss, it, 4 * g + 3)
            then(e.tensor_scalar(sx[:, :], x_, 1e-24, None, ALU.max))
            yield
            before()
            then(e.tensor_scalar(t.bitcast(I32), sx[:, :].bitcast(I32), 1, None, ALU.arith_shift_right))
            yield
            before()
            then(e.tensor_scalar(y_.bitcast(I32), t.bitcast(I32), -1.0, float(0x5F3759DF), ALU.mult, ALU.add))
            then(e.tensor_scalar(h, sx[:, :], -0.5, None, ALU.mult))
            yield
            for _ in range(NEWTON):
                before()
                then(e.tensor_tensor(t, y_, y_, ALU.mult))
                yield
                before()
                then(e.tensor_tensor(t, t, h, ALU.mult))
                yield
                before()
                then(e.scalar_tensor_tensor(y_, t, 1.5, y_, ALU.add, ALU.mult))
                yield

        def normalise(e, it, j):
            done(e, b_ad, it, j)
            done(e, b_rs, it, (j // 4) * NORM + NORM - 1)
            free(e, b_tr, it, j, 4)
            e.tensor_tensor(qn[:, j % 4, :].rearrange("p (h d) -> p h d", d=DB),
                            ra[:, j % 4, :].rearrange("p (h d) -> p h d", d=DB),
                            rs[:, j % 4, :].unsqueeze(2).to_broadcast([P, 8, DB]), ALU.mult)\
             .then_inc(b_qn.sem, 1)

        pW = [pP, pT]

        def turn(e, it, j):
            done(e, b_qn, it, j)
            if j % 4 < 2:
                done(e, b_pc, it, 2 * (j // 4) - 2 + j % 4)
            else:
                free(e, b_tc, it, j, 2)
            for p in range(4):
                i = e.transpose(pW[j % 2][:, p * P:(p + 1) * P], qn[:, j % 4, p * P:(p + 1) * P], ident)
            i.then_inc(b_tr.sem, 1)

        def turn_copy(e, it, j):
            g, t, isk = j // 4, (j % 4) // 2, j % 2
            done(e, b_tr, it, j)
            if j % 4 == 0:
                free(e, b_S, it, 2 * g + 1, UNITS)
            w = pW[j % 2]
            if isk:
                e.copy(kT[g][:, :, WIN + t * P:WIN + (t + 1) * P],
                       w[:, :].rearrange("p (h q) -> p h q", h=4)).then_inc(b_tc.sem, 1)
            else:
                for s in range(2):
                    i = e.copy(qd[g][64 * s:64 * s + 64, :, 4 * t:4 * t + 4, WIN * s:WIN * s + WIN],
                               w[64 * s:64 * s + 64, :].rearrange("p (h w q) -> p h w q", h=4, w=4))
                i.then_inc(b_tc.sem, 1)

        def scores(e, it, u):
            g, s = u // 2, u % 2
            done(e, b_tc, it, 4 * g + 3)
            free(e, b_sub, it, u, 2)
            e.matmul(pS[s][:, :], ident16[:, :], maskB[:, :], start=True, stop=False, skip_group_check=True)
            for p2 in range(2):
                for w in range(NW):
                    lo = p2 * 256 + (w // 2) * 64
                    i = e.matmul(pS[s][64 * (w % 2):64 * (w % 2) + 64, lo:lo + 64],
                                 qd[g][:, 2 * (u % 2) + p2, w, :],
                                 kT[g][:, 2 * (u % 2) + p2, WIN * w:WIN * w + 2 * WIN],
                                 start=False, stop=True, skip_group_check=True)
            i.then_inc(b_S.sem, 1)

        def less_max(e, it, u):
            s = u % 2
            done(e, b_S, it, u)
            sc = pS[s][:, :].rearrange("p (n k) -> p n k", k=64)
            e.tensor_reduce(mx[:, s, :], sc, AX.X, ALU.max).then_inc(b_mx.sem, 1)
            done(e, b_mx, it, u)
            free(e, b_ex, it, u, 2)
            e.tensor_tensor(dif[:, s, :].rearrange("p (n k) -> p n k", k=64), sc,
                            mx[:, s, :].unsqueeze(2).to_broadcast([P, 8, 64]), ALU.subtract)\
             .then_inc(b_sub.sem, 1)

        def exponent(e, it, u):
            s = u % 2
            done(e, b_sub, it, u)
            free(e, b_pt, it, u, 2)
            e.activation(pr[:, s, :], dif[:, s, :], ACT.Exp, scale=8.0).then_inc(b_ex.sem, 1)

        def row_sums(e, it, u):
            s = u % 2
            done(e, b_ex, it, u)
            e.tensor_reduce(sm[:, s, :], pr[:, s, :].rearrange("p (n k) -> p n k", k=64),
                            AX.X, ALU.add).then_inc(b_sm.sem, 1)
            done(e, b_sm, it, u)
            e.reciprocal(rl[:, s, :], sm[:, s, :]).then_inc(b_rl.sem, 1)

        def soft_norm(e, it, u):
            s = u % 2
            done(e, b_rl, it, u)
            y = pr[:, s, :].rearrange("p (n k) -> p n k", k=64)
            e.tensor_tensor(y, y, rl[:, s, :].unsqueeze(2).to_broadcast([P, 8, 64]), ALU.mult)\
             .then_inc(b_pn.sem, 1)

        def turn_p(e, it, u):
            done(e, b_pn, it, u)
            done(e, b_tc, it, 4 * (u // 2) + 2 + u % 2)
            for n in range(4):
                i = e.transpose(pW[u % 2][:, n * P:(n + 1) * P], pr[:, u % 2, n * P:(n + 1) * P], ident)
            i.then_inc(b_pt.sem, 1)

        def copy_p(e, it, u):
            done(e, b_pt, it, u)
            free(e, b_pv, it, 2 * u + 1, 4)
            dst = pt[:, u % 2, :, :, :, :].rearrange("p n a b k -> p (n a) b k")
            src = pW[u % 2][:, :].rearrange("p (n k) -> p n k", k=64)
            for h in range(2):
                i = e.copy(dst[64 * h:64 * h + 64, :, h, :], src[64 * h:64 * h + 64, :, :])
            i.then_inc(b_pc.sem, 1)

        def values(e, it, k, nxt=False):
            u, g, p2, pair = k // 2, k // 4, k % 2, k % 4
            if p2 == 0:
                done(e, b_pc, it, u)
            if pair == 0:
                done(e, b_ev, it, 2 * g + 1)
                done(e, b_vs[g], it)
            free(e, b_oc, it, k, 2)
            if k == 0:
                done(e, b_wx, it - 1)
            if k == 1 and nxt:
                done(e, b_xs, it + 1)
            o = pV[k % 2][:, :].rearrange("p (t a c q) -> p t a c q", t=NT, a=2, c=2)
            for t in range(NT):
                for par in range(2):
                    i = e.matmul(o[:, t, :, par, :], (v if par else vs)[g][:, t, pair * P:(pair + 1) * P],
                                 pt[:, u % 2, 2 * p2 + t, par, :, :], start=(t == 0 and par == 0), stop=True,
                                 skip_group_check=True)
            i.then_inc(b_pv.sem, 1)

        def copy_o(e, it, k):
            done(e, b_pv, it, k)
            if k == 0:
                free(e, b_wo, it, 0, 1)
            o = pV[k % 2][:, :].rearrange("p (w h q) -> p w h q", h=2, q=WIN)
            for h in range(2):
                i = e.copy(oT[64 * h:64 * h + 64, k, :].rearrange("p (w q) -> p w q", q=WIN),
                           o[64 * h:64 * h + 64, :, h, :])
            i.then_inc(b_oc.sem, 1)

        def out_proj(e, it):
            done(e, b_oc, it, PAIRS - 1)
            for t in range(NT):
                for k in range(PAIRS):
                    i = e.matmul(pO[:, t * M:(t + 1) * M], oT[:, k, t * P:(t + 1) * P], woB[:, k, :],
                                 start=(k == 0), stop=(k == PAIRS - 1))
            i.then_inc(b_wo.sem, 1)

        def out_add(e, it, b):
            done(e, b_wo, it)
            xd = xr[:, bass.ds(b * NT, NT), :]
            e.tensor_tensor(xd, pO[:, 0:T].rearrange("p (t m) -> p t m", t=NT), xd, ALU.add)\
             .then_inc(b_wx.sem, 1)

        def move_values(e, it, g):
            done(e, b_ev, it, 2 * g + 1)
            settle(e, e_hold)
            free(e, b_pv, it, 4 * g + 3, PAIRS)
            settle(e, e_hold)
            e.dma_start(vs[g][WIN:P, :, :], v[g][0:P - WIN, :, :]).then_inc(b_vs[g].sem, 16)
            e.dma_start(vs[g][0:WIN, 1, :], v[g][P - WIN:P, 0, :]).then_inc(b_vs[g].sem, 16)

        def slot(en, e, it, b, g, F_, K_, L_, nxt=False):
            ib, gb_ = (it, g - 1) if g else (it - 1, GROUPS - 1)
            il, gl = it - 1, g
            c0, j0 = 6 * g, 4 * g
            jb, u0 = 4 * gb_, 2 * gb_
            ul, kl = 2 * gl, 4 * gl
            steps = []
            F = lambda f, *a, on=True: steps.append((F_ and on, f, a))
            K = lambda f, *a, on=True: steps.append((K_ and on, f, a))
            L = lambda f, *a, on=True: steps.append((L_ and on, f, a))
            if en == "pe":
                L(turn_p, il, ul)
                F(proj, it, c0)
                F(proj, it, c0 + 1)
                L(turn_p, il, ul + 1)
                L(values, il, kl)
                K(turn, ib, jb)
                L(values, il, kl + 1, F_)
                K(turn, ib, jb + 1)
                F(proj, it, c0 + 2)
                K(turn, ib, jb + 2)
                L(values, il, kl + 2)
                F(proj, it, c0 + 3)
                K(turn, ib, jb + 3)
                L(values, il, kl + 3)
                K(scores, ib, u0)
                K(scores, ib, u0 + 1)
                F(xt_turn, it + 1, on=nxt)
                F(proj, it, c0 + 4)
                F(proj, it, c0 + 5)
                L(out_proj, il, on=g == 1)
            if en == "act":
                L(copy_p, il, ul)
                F(square, it, j0)
                F(square, it, j0 + 1)
                L(copy_p, il, ul + 1)
                L(copy_o, il, kl)
                K(turn_copy, ib, jb)
                L(copy_o, il, kl + 1)
                K(turn_copy, ib, jb + 1)
                F(square, it, j0 + 2)
                K(turn_copy, ib, jb + 2)
                L(copy_o, il, kl + 2)
                F(square, it, j0 + 3)
                K(turn_copy, ib, jb + 3)
                L(copy_o, il, kl + 3)
                K(exponent, ib, u0)
                F(move_v, it, c0 + 4)
                F(xt_shift, it + 1, on=nxt)
                K(exponent, ib, u0 + 1)
                F(move_v, it, c0 + 5)
            if en == "dve":
                chain = norm_chain(e, it, g)
                link = lambda *a: next(chain, None)

                def links(n):
                    for _ in range(n):
                        F(link)

                F(rotate, it, j0)
                F(rotate, it, j0 + 1)
                F(rotate, it, j0 + 2)
                F(rotate, it, j0 + 3)
                K(less_max, ib, u0)
                links(1)
                K(less_max, ib, u0 + 1)
                links(1)
                K(row_sums, ib, u0)
                links(3)
                K(row_sums, ib, u0 + 1)
                links(1)
                F(xt_low, it + 1, on=nxt)
                links(1)
                L(out_add, il, b - 1, on=g == 1)
                links(6)
            if en == "pool":
                F(rotate_add, it, j0)
                F(rotate_add, it, j0 + 1)
                F(xt_copy, it + 1, b + 1, on=nxt)
                F(rotate_add, it, j0 + 2)
                K(soft_norm, ib, u0)
                F(rotate_add, it, j0 + 3)
                K(soft_norm, ib, u0 + 1)
                F(normalise, it, j0)
                F(normalise, it, j0 + 1)
                F(normalise, it, j0 + 2)
                F(normalise, it, j0 + 3)
            for on, f, a in steps:
                if on:
                    f(e, *a)

        def b_pass(en, e, l, b, first=False, last=False):
            it = l * B + b
            slot(en, e, it, b, 0, True, not first, not first)
            slot(en, e, it, b, 1, True, True, not first, not last)

        def b_attention(en, e, l):
            if en == "pool":
                xt_copy(e, l * B, 0)
            if en == "pe":
                xt_turn(e, l * B)
            if en == "pe":
                done(e, b_wl, l)
                settle(e, e_hold)
            if en == "act":
                xt_shift(e, l * B)
            if en == "dve":
                xt_low(e, l * B)
            b_pass(en, e, l, 0, first=True)
            with e.Fori(1, B - 1) as b:
                b_pass(en, e, l, b)
            b_pass(en, e, l, B - 1, last=True)
            slot(en, e, (l + 1) * B, B, 0, False, True, True)

        def attention_to_feed_forward(en, e, l):
            il, nx = (l + 1) * B - 1, l * FP
            done(e, e_w1, l)
            settle(e, e_hold)
            if en == "pe":
                turn_p(e, il, 2)
                turn_p(e, il, 3)
                values(e, il, 4)
                values(e, il, 5)
                done(e, b_pc, il, 3)
                settle(e, e_hold)
                done(e, b_wx, l * B + 1)
                settle(e, e_hold)
                l_shift(e, nx, 0)
                values(e, il, 6)
                values(e, il, 7)
                out_proj(e, il)
                l_turn(e, nx)
            if en == "act":
                copy_p(e, il, 2)
                copy_p(e, il, 3)
                copy_o(e, il, 4)
                copy_o(e, il, 5)
                copy_o(e, il, 6)
                copy_o(e, il, 7)
            if en == "dve":
                l_second(e, nx)
                l_stats(e, nx, 0)
                done(e, f_st, nx, 1)
                for _ in rsqrt_chain(e, f_rs, nx, frs[:, :], fmv[:, :, 1], fnt):
                    pass
                done(e, b_tr, il, 7)
                l_norm(e, nx)
                out_add(e, il, B - 1)
                l_scale(e, nx)
            if en == "pool":
                done(e, b_wx, l * B + 1)
                settle(e, e_hold)
                l_first(e, nx, 0)
                l_bias(e, nx, 0)

        tiles = lambda f: bass.ds(f * FT, FT)

        def l_shift(e, it, f):
            free(e, f_xs, it, 0, 1)
            e.matmul(pP[:, 0:FT * HALF], down, xr[:, tiles(f), HALF:M], start=True, stop=False,
                     skip_group_check=True)
            o = pP[:, 0:FT * HALF].rearrange("p (b t m) -> p b t m", t=NT, m=HALF)
            e.matmul(o[:, :, 1, :], wrap, xr[:, tiles(f), HALF:M].rearrange("p (b t) m -> p b t m", t=NT)[:, :, 0, :],
                     start=False, stop=True, skip_group_check=True).then_inc(f_sh.sem, 1)

        def l_first(e, it, f):
            free(e, f_ln, it, 0, 1)
            settle(e, e_hold)
            e.tensor_copy(fx[:, :, 0:HALF], xr[:, tiles(f), 0:HALF]).then_inc(f_xa.sem, 1)

        def l_second(e, it):
            done(e, f_sh, it)
            free(e, f_ln, it, 0, 1)
            e.tensor_copy(fx[:, :, HALF:M], pP[:, 0:FT * HALF].rearrange("p (t m) -> p t m", m=HALF)).then_inc(f_xs.sem, 1)

        def l_stats(e, it, f):
            done(e, f_xa, it)
            settle(e, e_hold)
            done(e, f_xs, it)
            settle(e, e_hold)
            moments(e, f_st, it, fst, fmv, [fx[:, t, :] for t in range(FT)])

        def l_norm(e, it):
            done(e, f_rs, it, FNORM - 1)
            free(e, f_lt, it, 0, 1)
            for t in range(FT):
                i = e.tensor_scalar(fln[:, t, :], fx[:, t, :], fmv[:, t, 0:1], frs[:, t:t + 1],
                                    ALU.subtract, ALU.mult)
            i.then_inc(f_ln.sem, 1)

        def l_bias(e, it, f):
            done(e, f_sh, it)
            settle(e, e_hold)
            done(e, f_xa, it)
            settle(e, e_hold)
            xd = xr[:, tiles(f), :]
            e.tensor_tensor(xd, xd, b2b[:, :, :].to_broadcast([P, FT, M]), ALU.add).then_inc(f_xb.sem, 1)

        def l_turn(e, it):
            done(e, f_ln, it)
            free(e, f_xn, it, 0, 1)
            for t in range(FT):
                i = e.transpose(pT[:, t * P:(t + 1) * P], fln[:, t, :], ident)
            i.then_inc(f_lt.sem, 1)

        def l_scale(e, it):
            done(e, f_lt, it)
            free(e, f_h, it, 2, 3)
            e.tensor_scalar(xnT, pT[:, :], lng[:, 0:1], lnb[:, 0:1], ALU.mult, ALU.add)\
             .then_inc(f_xn.sem, 1)

        def m_hidden(e, it, n):
            k = FCH[n]
            if n == 0:
                done(e, f_xn, it)
            done(e, f_G, it, (-1, -2, 0)[n])
            for h, bk in ((1, pS), (0, pQ)):
                i = e.matmul(bk[n % 2][0:k, :], w1[:, h * F + n * P:h * F + n * P + k], xnT,
                             start=True, stop=True)
            i.then_inc(f_h.sem, 1)

        def m_warm(e):
            e.activation(warm[:, 1:2], warm[:, 0:1], ACT.Gelu)

        def m_gelu(e, it, n):
            k = FCH[n]
            done(e, f_h, it, n)
            done(e, f_G, it, n - 2 if n else -1)
            e.activation(gel[0:k, n % 2, :], pS[n % 2][0:k, :], ACT.Gelu, bias=b1c[0:k, 1, n:n + 1])\
             .then_inc(f_ge.sem, 1)

        def m_gate(e, it, n):
            k = FCH[n]
            done(e, f_ge, it, n)
            free(e, f_y, it, n, 3)
            e.scalar_tensor_tensor(gT[0:k, n, :], pQ[n % 2][0:k, :], b1c[0:k, 0, n:n + 1], gel[0:k, n % 2, :],
                                   ALU.add, ALU.mult).then_inc(f_G.sem, 1)

        def m_out(e, it, n):
            k = FCH[n]
            done(e, f_G, it, n)
            if n == 0:
                free(e, f_x, it, 0, 1)
            for t in range(FT):
                i = e.matmul(pO[:, t * P:(t + 1) * P], gT[0:k, n, t * P:(t + 1) * P], w2[0:k, n, :],
                             start=(n == 0 and t == 0), stop=(n == 2), skip_group_check=True)
            i.then_inc(f_y.sem, 1)

        def m_add(e, it, f):
            done(e, f_xb, it)
            done(e, f_y, it, 2)
            xd = xr[:, tiles(f), :]
            e.tensor_tensor(xd, pO[:, :].rearrange("p (t m) -> p t m", t=FT), xd, ALU.add).then_inc(f_x.sem, 1)

        def f_slot(en, e, it, f, M_, L_):
            steps = []
            m = lambda fn, *a: steps.append((M_, fn, a))
            n_ = lambda fn, *a: steps.append((L_, fn, a))
            nx = it + 1
            if en == "pe":
                n_(l_shift, nx, f + 1)
                m(m_hidden, it, 0)
                m(m_hidden, it, 1)
                m(m_out, it, 0)
                m(m_hidden, it, 2)
                m(m_out, it, 1)
                n_(l_turn, nx)
                m(m_out, it, 2)
            if en == "act":
                m(m_warm)
                for n in range(3):
                    m(m_gelu, it, n)
            if en == "dve":
                chain = rsqrt_chain(e, f_rs, nx, frs[:, :], fmv[:, :, 1], fnt)
                link = lambda *a: next(chain, None)
                n_(l_second, nx)
                n_(l_stats, nx, f + 1)
                n_(done, f_st, nx, 1)
                n_(link)
                m(m_gate, it, 0)
                for _ in range(5):
                    n_(link)
                m(m_gate, it, 1)
                for _ in range(7):
                    n_(link)
                n_(l_norm, nx)
                m(m_gate, it, 2)
                n_(l_scale, nx)
                m(m_add, it, f)
            if en == "pool":
                n_(l_first, nx, f + 1)
                n_(l_bias, nx, f + 1)
            for on, fn, a in steps:
                if on:
                    fn(e, *a)

        def b_feed_forward(en, e, l):
            with e.Fori(0, FP - 1) as f:
                f_slot(en, e, l * FP + f, f, True, True)
            split_weights(en, e, l + 1)
            f_slot(en, e, l * FP + (FP - 1), FP - 1, True, False)

        def run(en, e):
            done(e, e_set, 0)
            if en == "pe":
                e.transpose(pM[:, 0:B], cr[:, :], eye[0:B, 0, 0:B]).then_inc(a_cT.sem, 1)
            if en == "act":
                done(e, a_cT, 0)
                e.activation(cT[:, 1, :], pM[:, 0:B], ACT.Exp, scale=-1.0)
                e.copy(cT[:, 0, :], pM[:, 0:B]).then_inc(a_e.sem, 1)
            if en == "dve":
                done(e, a_e, 0)
                e.tensor_scalar(cT[:, 1, :], cT[:, 1, :], 1.0, None, ALU.add).then_inc(a_si.sem, 1)
                done(e, a_si, 0, 0)
                e.reciprocal(cT[:, 2, :], cT[:, 1, :]).then_inc(a_si.sem, 1)
                done(e, a_si, 0, 1)
                e.tensor_tensor(cT[:, 3, :], cT[:, 0, :], cT[:, 2, :], ALU.mult).then_inc(a_si.sem, 1)
            if en == "pe":
                done(e, a_si, 0, 2)
                for n in range(2):
                    i = e.matmul(pO[:, n * B:(n + 1) * B], wm[:, n * M:(n + 1) * M], cT[:, 3, :],
                                 start=True, stop=True)
                i.then_inc(a_mt.sem, 1)
            if en == "dve":
                done(e, a_mt, 0)
                e.tensor_scalar(s1T[:, :, 0], pO[:, B:2 * B], 1.0, None, ALU.add)
                e.tensor_copy(s1T[:, :, 1], pO[:, 0:B])
            barrier(e, 0)
            part_a(en, e)
            barrier(e, 1)
            if en == "dve":
                for g in range(GROUPS):
                    i = e.memset(qd[g][:, :, :, :], 0.0)
                i.then_inc(b_z.sem, 1)
            if en == "act":
                done(e, b_z, 0)
                settle(e, e_hold)
            with e.Fori(0, DEPTH) as l:
                done(e, e_wq, l)
                if en == "dve":
                    e.tensor_tensor(rope[:, :, :, :], ropeB[:, :, :, :],
                                    qks[:, :, :].unsqueeze(1).to_broadcast([P, NT, 4, DB]), ALU.mult)\
                     .then_inc(b_rp.sem, 1)
                    done(e, b_rp, l)
                    settle(e, e_hold)
                b_attention(en, e, l)
                attention_to_feed_forward(en, e, l)
                barrier(e, l * 2 + 2)
                b_feed_forward(en, e, l)
                barrier(e, l * 2 + 3)
            if en == "dve":
                for b0 in range(0, 2):
                    lo, hi = b0 * B // 2, (b0 + 1) * B // 2
                    y = xr[:, lo * NT:hi * NT, :].rearrange("p (b t) m -> p b t m", t=NT)
                    e.tensor_tensor(y, y, gb[:, lo:hi, :].unsqueeze(2).to_broadcast([P, B // 2, NT, M]),
                                    ALU.mult).then_inc(o_m.sem, 1)
                done(e, o_m, 0, 1)
                e.tensor_tensor(x1[:, :, :], x1[:, :, :], xr[:, :, :], ALU.add).then_inc(o_m.sem, 1)

        def load_layer_attention(e, l):
            row = lambda a, n: a[bass.ds(l, 1), n].to_broadcast([P, n.stop - n.start])
            lo, hi, full = slice(0, DB // 2), slice(DB // 2, DB), slice(0, DB)
            e.dma_start(wqkvB[:, :, :], Wqkv[bass.ds(l, 1), :, :].rearrange("o m (n c) -> (o m) n c", n=3))\
             .then_inc(e_wq.sem, 16)
            e.dma_start(woB[:, :, :], Wo[bass.ds(l, 1), :, :].rearrange("o (k p) m -> p (o k) m", p=P))\
             .then_inc(e_wq.sem, 16)
            for n, a in enumerate((q_scale, k_scale)):
                e.dma_start(qks[:, 2 * n, full], row(a, full)).then_inc(e_wq.sem, 16)
                e.dma_start(qks[:, 2 * n + 1, lo], row(a, hi)).then_inc(e_wq.sem, 16)
                e.dma_start(qks[:, 2 * n + 1, hi], row(a, lo)).then_inc(e_wq.sem, 16)

        def load_layer_feed_forward(e, l):
            e.dma_start(w1[:, :], W1[bass.ds(l, 1), :, :].rearrange("o m f -> (o m) f")).then_inc(e_w1.sem, 16)
            for n in range(3):
                k = min(P, F - n * P)
                e.dma_start(w2[0:k, n, :], W2[bass.ds(l, 1), n * P:n * P + k, :].rearrange("o f m -> (o f) m"))\
                 .then_inc(e_w1.sem, 16)
            for n, k in enumerate(FCH):
                for h in range(2):
                    lo = h * F + n * P
                    e.dma_start(b1c[0:k, h, n:n + 1], b1[bass.ds(l, 1), lo:lo + k].rearrange("o f -> f o"))\
                     .then_inc(e_w1.sem, 16)
            e.dma_start(b2b[:, 0, :], b2[bass.ds(l, 1), :].to_broadcast([P, M])).then_inc(e_w1.sem, 16)
            e.dma_start(lng[:, :], ln_g[bass.ds(l, 1), :].rearrange("o m -> m o")).then_inc(e_w1.sem, 16)
            e.dma_start(lnb[:, :], ln_b[bass.ds(l, 1), :].rearrange("o m -> m o")).then_inc(e_w1.sem, 16)

        @block.sync
        def _(e):
            for x_ in events:
                if x_.credit:
                    e.sem_inc(x_.sem, x_.credit)
            e.dma_start(x0[:, :, :], x.rearrange("b (t p) m -> p (b t) m", p=P)).then_inc(e_const.sem, 16)
            for n, w in enumerate((wq, wk, wv)):
                e.dma_start(wqkvA[:, n, :], w.rearrange("m h d -> m (h d)")).then_inc(e_const.sem, 16)
            e.dma_start(woA[:, :, :], wo.rearrange("h d m -> d h m")).then_inc(e_const.sem, 16)
            for dst, src in ((ropeA[:, :, :, :], ropeA_in), (ropeB[:, :, :, :], ropeB_in), (eye[:, :, :], eye_in),
                             (mask_f[:, :, :], masks_in), (cr[:, :], c), (wm[:, :], wmod)):
                e.dma_start(dst, src).then_inc(e_const.sem, 16)
            done(e, a_pj, B - 1, NCH - 1)
            with e.Fori(0, DEPTH) as l:
                e.wait_ge(e_bar.sem, l * 8 + 4)
                settle(e, e_hold)
                load_layer_attention(e, l)
                e.wait_ge(e_bar.sem, l * 8 + 8)
                settle(e, e_hold)
                load_layer_feed_forward(e, l)
                with e.Fori(0, B) as b:
                    for g in range(GROUPS):
                        move_values(e, l * B + b, g)
            e.sem_inc(e_wq.sem, e_wq.step)
            done(e, o_m, 0, 2)
            e.dma_start(out.rearrange("b (t p) m -> p (b t) m", p=P), x1[:, :, :]).then_inc(o_out.sem, 16)
            done(e, o_out, 0)

        @block.gpsimd
        def _(e):
            run("pool", e)

        @block.vector
        def _(e):
            e.memset(warm[:, :], 0.0)
            e.memset(pt[:, :, :, :, :, :], 0.0)
            for g in range(GROUPS):
                e.memset(kT[g][:, :, 0:WIN], 0.0)
                e.memset(vs[g][0:WIN, 0, :], 0.0)
            done(e, e_const, 0)
            for y in (xsh, xsl):
                e.tensor_copy(y[HALF:P, 0:1], eye[HALF:P, 0, 0:1])
            e.tensor_copy(ident16[:, :], ident)
            e.tensor_copy(maskA[:, :], mask_f[:, 0, 0:3 * P])
            e.tensor_copy(maskB[:, :], mask_f[:, 1, :]).then_inc(e_set.sem, 1)
            run("dve", e)

        @block.scalar
        def _(e):
            run("act", e)

        @block.tensor
        def _(e):
            run("pe", e)


def tables():
    f = np.float32
    pos = np.arange(T, dtype=f)

    half = DA // 2
    freq = np.power(f(10000.0), (-np.arange(half) / f(half)).astype(f)).astype(f)
    rad = (pos[:, None] * freq[None, :]).astype(f)
    c, s = np.cos(rad).astype(f), np.sin(rad).astype(f)
    ropeA = np.stack([np.concatenate([c, c], -1), np.concatenate([-s, s], -1)], 1)
    hb = np.arange(0, DB, 2, dtype=f)
    inv = (f(1.0) / np.power(f(10000.0), hb / f(DB))).astype(f)
    rad = (pos[:, None] * inv[None, :]).astype(f)
    c, s = np.cos(rad).astype(f), np.sin(rad).astype(f)
    base = ((hb + f(0.4 * DB)) / f(1.4 * DB)).astype(f)
    power = ((pos - T // 2) / f(WIN // 2)).astype(f)
    sc = np.power(base[None, :], power[:, None]).astype(f)
    iv = (f(1.0) / sc).astype(f)
    cat = lambda a, b: np.concatenate([a, b], -1)
    ropeB = np.stack([cat(c * sc, c * sc), cat(-s * sc, s * sc), cat(c * iv, c * iv), cat(-s * iv, s * iv)], 1)
    lay = lambda a: np.ascontiguousarray(a.reshape(NT, P, *a.shape[1:]).transpose(1, 0, 2, 3).astype(f))
    q, k = np.arange(P)[:, None], np.arange(P)[None, :]
    diag = np.where(q < k, f(NEG), f(0))
    maskA = np.concatenate([diag, np.zeros((P, P), f), diag, np.zeros((P, P), f)], 1)
    maskB = np.zeros((2, 2, WIN, 2, NW // 2, 2 * WIN), f)
    r, kk = np.arange(WIN)[:, None], np.arange(2 * WIN)[None, :]
    band = np.where((kk < r) | (kk > r + WIN), f(NEG), f(0))
    maskB += band[None, None, :, None, None, :]
    maskB[0, :, :, :, 0, :WIN] = NEG
    masks = np.ascontiguousarray(np.stack([maskA, maskB.reshape(P, CH)], 1).astype(f))
    eye = np.stack([np.eye(P, dtype=f), np.eye(P, k=1, dtype=f), np.eye(P, k=1 - P, dtype=f)], 1)
    return np.ascontiguousarray(eye), masks, lay(ropeA), lay(ropeB)


_INS = ["L0_attn_x", "L0_attn_wq", "L0_attn_wk", "L0_attn_wv", "L0_attn_wo", "L0_ffn_Wqkv", "L0_ffn_q_scale",
        "L0_ffn_k_scale", "L0_ffn_Wo", "L0_ffn_ln_g", "L0_ffn_ln_b", "L0_ffn_W1", "L0_ffn_b1", "L0_ffn_W2",
        "L0_ffn_b2", "L0_c", "L0_wmod"]


def kernel(**inputs):
    import concourse.bacc as bacc
    from concourse.bass_utils import run_bass_kernel_spmd

    nc = bacc.Bacc("TRN2", target_bir_lowering=False, num_devices=1)
    arrays = {name: np.ascontiguousarray(inputs[name]) for name in _INS}
    for name, table in zip(("eye", "masks", "rope_a", "rope_b"), tables()):
        arrays[name] = table
    args = []
    for name, a in arrays.items():
        args.append(nc.dram_tensor(f"in_{name}", a.shape, mybir.dt.from_np(a.dtype), kind="ExternalInput").ap())
    args.append(nc.dram_tensor("out_0", (B, T, M), F32, kind="ExternalOutput").ap())
    build(nc, *args)
    r = run_bass_kernel_spmd(nc, [{f"in_{n}": a for n, a in arrays.items()}], core_ids=[0])
    return r.results[0]["out_0"]
```
